# Optimizing a Trainium2 kernel written in Bass

```python
import numpy as np
import jax
import jax.numpy as jnp

def _softmax(x, axis=-1):
    return jax.nn.softmax(x, axis=axis)

def _gelu(x):
    return jax.nn.gelu(x, approximate=True)

def _silu(x):
    return jax.nn.silu(x)

def _sigmoid(x):
    return jax.nn.sigmoid(x)

def _layernorm(x, axis=-1, eps=1e-05):
    m = jnp.mean(x, axis=axis, keepdims=True)
    v = jnp.var(x, axis=axis, keepdims=True)
    return (x - m) / jnp.sqrt(v + eps)

def _scatter_add(tgt, idx, src, axis=0):
    return tgt.at[idx].add(src)

def _segment_sum(src, seg, n):
    return jax.ops.segment_sum(src, seg, n)
kernel_name = 'mk_adj_resnorm_d2_adj_r2_045272'

def setup_inputs(seed: int=0):
    np.random.seed(seed)
    _w = jnp.asarray

    def _rec_inputs():
        import jax
        import jax.numpy as jnp
        _gk = jax.random.key(seed)
        x = 4.136e-05 + 0.9999 * jax.random.normal(jax.random.fold_in(_gk, 1), (4096, 256), jnp.float32)
        _w = (1.0 + jnp.arange(4096, dtype=jnp.float32)) ** (-0.5)
        _w = _w / _w.mean()
        _pij = jnp.clip(0.000488281 * _w[:, None] * _w[None, :], 0.0, 1.0)
        _a = jax.random.uniform(jax.random.fold_in(_gk, 2), (4096, 4096)) < _pij
        _a = jnp.logical_or(_a, jnp.swapaxes(_a, -1, -2))
        _af = _a.astype(jnp.float32)
        adj = _af
        return (x, adj)
    x, adj = _rec_inputs()

    def _L0_gnn_setup():
        import jax, jax.numpy as jnp
        import numpy as np
        N = 8192
        D_IN = 256
        D_OUT = 256
        AVG_DEG = 32.0
        key = jax.random.key(seed)
        k1, k2, k3, k4 = jax.random.split(key, 4)
        p = AVG_DEG / N
        adjacency = (jax.random.uniform(k1, (N, N)) < p).astype(jnp.float32)
        adjacency = jnp.maximum(adjacency, adjacency.T)
        node_degree = jnp.sum(adjacency, axis=1, keepdims=True) + 1.0
        x = jax.random.normal(k2, (N, D_IN), dtype=jnp.float32)
        W = jax.random.normal(k3, (D_IN, D_OUT), dtype=jnp.float32) * (1.0 / np.sqrt(D_IN))
        b = jax.random.normal(k4, (D_OUT,), dtype=jnp.float32) * 0.01
        return {'x': x, 'adjacency': adjacency, 'node_degree': node_degree, 'W': W, 'b': b}
    _L0_gnn_all = _L0_gnn_setup()
    _L0_gnn_in = {k: v for k, v in _L0_gnn_all.items() if k in ('W', 'b')}
    del _L0_gnn_all

    def _L1_gnn_setup():
        import jax, jax.numpy as jnp
        import numpy as np
        N = 3072
        D_IN = 256
        D_OUT = 256
        DENSITY = 0.005
        key = jax.random.key(seed)
        ks = jax.random.split(key, 12)
        x = jax.random.normal(ks[0], (N, D_IN), dtype=jnp.float32)
        adj_a = (jax.random.uniform(ks[1], (N, N)) < DENSITY).astype(jnp.float32)
        adj_b = (jax.random.uniform(ks[2], (N, N)) < DENSITY).astype(jnp.float32)
        W_sa = jax.random.normal(ks[3], (D_IN, D_OUT), dtype=jnp.float32) * (1.414 / np.sqrt(D_IN + D_OUT))
        a_sa = jax.random.normal(ks[4], (1, 2 * D_OUT), dtype=jnp.float32) * (1.414 / np.sqrt(1 + 2 * D_OUT))
        stdv = 1.0 / np.sqrt(D_OUT)
        W_gcnb = jax.random.uniform(ks[5], (D_IN, D_OUT), minval=-stdv, maxval=stdv, dtype=jnp.float32)
        b_gcnb = jax.random.uniform(ks[6], (D_OUT,), minval=-stdv, maxval=stdv, dtype=jnp.float32)
        s = 1.0 / np.sqrt(2 * D_IN)
        Wa = jax.random.uniform(ks[7], (1, 2 * D_IN), minval=-s, maxval=s, dtype=jnp.float32)
        ba = jax.random.uniform(ks[8], (1,), minval=-s, maxval=s, dtype=jnp.float32)
        Wb = jax.random.uniform(ks[9], (1, 2 * D_IN), minval=-s, maxval=s, dtype=jnp.float32)
        bb = jax.random.uniform(ks[10], (1,), minval=-s, maxval=s, dtype=jnp.float32)
        return {'x': x, 'adj_a': adj_a, 'adj_b': adj_b, 'W_sa': W_sa, 'a_sa': a_sa, 'W_gcnb': W_gcnb, 'b_gcnb': b_gcnb, 'Wa': Wa, 'ba': ba, 'Wb': Wb, 'bb': bb}
    _L1_gnn_all = _L1_gnn_setup()
    _L1_gnn_in = {k: v for k, v in _L1_gnn_all.items() if k in ('W_sa', 'a_sa', 'W_gcnb', 'b_gcnb', 'Wa', 'ba', 'Wb', 'bb')}
    del _L1_gnn_all
    return {'x': x, 'adj': adj, 'L0_gnn_W': _L0_gnn_in['W'], 'L0_gnn_b': _L0_gnn_in['b'], 'L1_gnn_W_sa': _L1_gnn_in['W_sa'], 'L1_gnn_a_sa': _L1_gnn_in['a_sa'], 'L1_gnn_W_gcnb': _L1_gnn_in['W_gcnb'], 'L1_gnn_b_gcnb': _L1_gnn_in['b_gcnb'], 'L1_gnn_Wa': _L1_gnn_in['Wa'], 'L1_gnn_ba': _L1_gnn_in['ba'], 'L1_gnn_Wb': _L1_gnn_in['Wb'], 'L1_gnn_bb': _L1_gnn_in['bb']}

def reference(x, adj, L0_gnn_W, L0_gnn_b, L1_gnn_W_sa, L1_gnn_a_sa, L1_gnn_W_gcnb, L1_gnn_b_gcnb, L1_gnn_Wa, L1_gnn_ba, L1_gnn_Wb, L1_gnn_bb):
    import jax
    import jax.numpy as jnp

    def _L0_gnn_ref(x, adjacency, node_degree, W, b):
        import jax, jax.numpy as jnp
        import numpy as np
        N = 8192
        D_IN = 256
        D_OUT = 256
        AVG_DEG = 32.0
        n = adjacency.shape[0]
        a_hat = adjacency + jnp.eye(n, dtype=adjacency.dtype)
        dinv = jax.lax.rsqrt(node_degree)
        a_norm = dinv * a_hat * dinv
        pooled = a_norm @ x + x
        return jax.nn.relu(pooled @ W + b)

    def _L1_gnn_ref(x, adj_a, adj_b, W_sa, a_sa, W_gcnb, b_gcnb, Wa, ba, Wb, bb):
        import jax, jax.numpy as jnp
        import numpy as np
        N = 3072
        D_IN = 256
        D_OUT = 256
        DENSITY = 0.005
        type_sum_a = adj_a @ x
        type_sum_b = adj_b @ x
        attn_a = jax.nn.sigmoid(jnp.concatenate([type_sum_a, x], axis=1) @ Wa.T + ba)
        attn_b = jax.nn.sigmoid(jnp.concatenate([type_sum_b, x], axis=1) @ Wb.T + bb)
        h = x @ W_sa
        Hd = h.shape[1]
        s_left = h @ a_sa[0, :Hd]
        s_right = h @ a_sa[0, Hd:]
        scores = s_left[:, None] + s_right[None, :]
        e = jnp.where(adj_a != 0, jnp.exp(-jax.nn.leaky_relu(scores, 0.01)), 0.0)
        attn = e / (jnp.sum(e, axis=1, keepdims=True) + 1e-05)
        x_a = attn @ h
        x_b = adj_b @ (x @ W_gcnb) + b_gcnb
        return jax.nn.sigmoid(attn_a * x_a + attn_b * x_b)
    deg = jnp.maximum((adj != 0).astype(jnp.float32).sum(-1), 1.0)
    x = _layernorm(x + _L0_gnn_ref(x, adj, deg[..., None], L0_gnn_W, L0_gnn_b), axis=-1)
    x = _layernorm(x + _L1_gnn_ref(x, adj, adj, L1_gnn_W_sa, L1_gnn_a_sa, L1_gnn_W_gcnb, L1_gnn_b_gcnb, L1_gnn_Wa, L1_gnn_ba, L1_gnn_Wb, L1_gnn_bb), axis=-1)
    return x

_drawn_inputs = setup_inputs


def setup_inputs(seed=0):
    import zlib

    import numpy as np

    out = dict(_drawn_inputs(seed))
    spreads = {}
    factors = {'L0_gnn_b': 8.0, 'L1_gnn_b_gcnb': 8.0}
    for name, (base, spread) in spreads.items():
        noise = np.random.default_rng([zlib.crc32(name.encode()), seed]).standard_normal(out[name].shape)
        drawn = base * np.exp(spread * noise) if base else spread * noise
        out[name] = jnp.asarray(drawn.astype(out[name].dtype))
    for name, factor in factors.items():
        out[name] = (out[name] * factor).astype(out[name].dtype)
    return out
```

```python
from contextlib import ExitStack

import numpy as np
import concourse.bass as bass
from concourse import mybir

ALU = mybir.AluOpType
ACT = mybir.ActivationFunctionType
AX = mybir.AxisListType.X
F32, F16, F8, U8 = mybir.dt.float32, mybir.dt.float16, mybir.dt.float8e4, mybir.dt.uint8
RMAX = bass.bass_isa.ReduceOp.max

P = 128
N = 4096
D = 256
T = N // P
KD = D // P
PW = 256
NPAN = N // PW
LOWP = NPAN // 2
GW = 512
TG = GW // P
NG = N // GW
NG2 = NG // 2
RING = 4
GC = D + 2
HC = D + 1
NEX = 4
WG = GC + NEX
WC = WG + D
EPS = 1e-5
F16_TOP = 32768.0
KAPPA = 16384.0
P_TOP = 80.0

BASE = 16512
O_FA = 0
O_FB = O_FA + T * 2 * GC * 2
O_FC = O_FB + T * 2 * HC * 2
O_Y = O_FB
O_X = O_Y + T * 2 * D * 2
O_HB = O_FC + T * 2 * HC * 2
O_RES = O_HB + T * D * 4
O_PERS = O_RES + T * N // 2
TOP = 229344 - BASE


class Steps:

    def __init__(self, eng, sem):
        self.eng, self.sem, self.n, self.base = eng, sem, 0, 0

    def then(self, ins):
        ins.then_inc(self.sem, 1)
        self.n += 1

    def sync(self):
        self.eng.wait_ge(self.sem, self.n + self.base)


def build(nc, x, adj, W0, b0, Wsa, asa, Wg, bg, Wa, ba, Wb, bb, out):
    def at(name, shape, dt, off):
        size = int(np.prod(shape[1:])) * mybir.dt.size(dt)
        assert off + size <= TOP, (name, off + size, TOP)
        return nc.alloc_sbuf_tensor_at(name, shape, dt, offset=BASE + off)

    class Area:

        def __init__(self, off, end):
            self.off, self.end = off, end

        def __call__(self, name, shape, dt):
            t = at(name, shape, dt, self.off)
            self.off += -(-int(np.prod(shape[1:])) * mybir.dt.size(dt) // 32) * 32
            assert self.off <= self.end, (name, self.off, self.end)
            return t

    class Area:

        def __init__(self, off, end):
            self.off, self.end = off, end

        def __call__(self, name, shape, dt):
            t = at(name, shape, dt, self.off)
            self.off += -(-int(np.prod(shape[1:])) * mybir.dt.size(dt) // 32) * 32
            assert self.off <= self.end, (name, self.off, self.end)
            return t

    fa = at("fa", [P, T, 2, GC], F16, O_FA)
    fb = at("fb", [P, T, 2, HC], F16, O_FB)
    fc = at("fc", [P, T, 2, HC], F16, O_FC)
    y = at("y", [P, T, 2, D], F16, O_Y)
    xs = at("xs", [P, T, D], F32, O_X)
    strip = at("strip", [P, RING, N // 2], F32, O_HB)
    h = at("h", [P, T, D], F32, O_HB)
    bm = at("bm", [P, 2, T, PW], F8, O_HB)
    cm = at("cm", [P, 2, T, PW], F8, O_HB + 2 * T * PW)
    res = at("res", [P, LOWP, T, PW], F8, O_RES)
    low = at("low", [P, 2, LOWP, 2, PW], F8, O_FA)
    area = Area(O_FA + 8192, O_FB)
    wsq = area("wsq", [P, KD, WC], F32)
    asab = area("asab", [P, 2 * D], F32)
    wtmp = area("wtmp", [P, D], F32)
    ones = area("ones", [P, P], F32)
    acct = [at(f"acct{g}", [P, KD, GW], F32, O_FA + 8192 + g * KD * GW * 4) for g in range(NG2)]
    area = Area(O_Y, O_X)
    acct += [area(f"acct{g}", [P, KD, GW], F32) for g in range(NG2, NG)]
    zx = area("zx", [P, 2, D], F32)
    x1t = area("x1t", [P, 2, KD, P], F32)
    lnst = area("lnst", [P, 2, 12], F32)
    pan = at("pan", [P, 2, T, PW], F8, O_RES)
    area = Area(O_RES + 3 * T * PW, O_PERS)
    slb = area("slb", [P, 2, PW], F32)
    x1r = area("x1r", [P, 2, D], F32)
    w = area("w", [P, 2, D], F32)
    wb = area("wb", [P, 2, D], F32)
    sg = area("sg", [P, 2, D], F32)
    ot = area("ot", [P, 2, D], F32)
    nsr = area("nsr", [P, T], F32)
    slc = area("slc", [P, T], F32)
    tq = area("tq", [P, T], F32)
    tp = area("tp", [P, T], F32)
    tpc = area("tpc", [P, T], F32)
    q = area("q", [P, T], F32)
    qp = area("qp", [P, T], F32)
    qa = area("qa", [P, T], F32)
    qpa = area("qpa", [P, T], F32)
    pp = area("pp", [P, T, 2], F32)
    rab = area("rab", [P, T, 2], F32)
    slrow = area("slrow", [T, P], F32)
    sc1 = area("sc1", [P, 2, 32], F32)
    area = Area(O_PERS, TOP)
    wp = area("wp", [P, KD, WC], F32)
    w0 = area("w0", [P, KD, D], F32)
    b0b = area("b0b", [P, D], F32)
    bgb = area("bgb", [P, D], F32)
    ident = area("ident", [P, P], F32)
    ex = area("ex", [P, T, NEX], F32)
    degv = area("degv", [P, T], F32)
    dega = area("dega", [P, T], F32)
    deg = area("deg", [P, T], F32)
    zs = area("zs", [P, T], F32)
    us = area("us", [P, T], F32)
    sc = area("sc", [P, 32], F32)
    (XM, SX, ISX, MH, ONE, NM, NMAX, XMX, WN, AL, INVA, BAB, TMP) = (
        slice(0, 4), slice(4, 5), slice(5, 6), slice(6, 7), slice(7, 8), slice(8, 9), slice(9, 10),
        slice(10, 11), slice(11, 12), slice(12, 13), slice(13, 14), slice(14, 16), slice(16, 18))
    XALL, XG, WMX = slice(18, 19), slice(19, 20), slice(20, 21)
    BN, MV, VE, RS, ATT, DD, D1, D2, REC, CI, CBC = (
        slice(0, 6), slice(6, 8), slice(8, 9), slice(9, 10), slice(10, 12), slice(12, 13), slice(13, 14),
        slice(14, 15), slice(15, 16), slice(16, 17), slice(17, 19))

    a8d = nc.dram_tensor("a8_scratch", [NPAN, P, T, PW], U8)
    x1d = nc.dram_tensor("x1_scratch", [N, D], F32)
    sld = nc.dram_tensor("sl_scratch", [N], F32)

    with ExitStack() as ctx:
        ps = ctx.enter_context(nc.psum_tensor("ps", [P, 8, 512], F32))
        block_sem = lambda name: ctx.enter_context(nc.semaphore(name))
        S = {}
        for name in (
            "x_in0", "x_in1", "x_in2", "x_in3", "wts_in", "wts_ready", "wsq_ready", "wsum_ready", "wnorm_ready",
            "alpha_pow", "const_ready", "xmax_part", "xmax_all", "sx_ready", "strip_in0", "strip_in1",
            "strip_in2", "strip_in3", "lo_cast", "hi_cast", "scale_ready", "yhi_ready", "ylo_ready",
            "strip_used", "low_out0", "low_out1", "res_out", "zx_ready", "zt_done", "acct_ready", "evac_act", "evac_dve",
            "u_done", "r2_done", "stat_ready", "rstd_ready", "x1_ready", "x1t_done", "x1t_ready", "proj_done",
            "ghi_ready", "h_ready", "glo_ready", "x1_out", "m_done", "nsr_max", "nmax_ready", "arg_ready",
            "pq_ready", "sl_ready", "slt_done", "slrow_ready", "sl_out", "qa_ready", "fbhi_ready", "fchi_ready",
            "feat_ready", "panel_in0", "panel_in1", "slb_in0", "slb_in1", "mask_ready", "a_done", "bc_done",
            "att_ready", "w_ready", "wb_ready", "epi_read", "sg_ready", "ystat_ready", "yrstd_ready", "out_ready",
            "x1r_in0", "x1r_in1", "out_sent0", "out_sent1", "dve_step", "pool_step", "passed_pe", "passed_dve",
            "passed_act", "passed_sp", "passed_pool", "x1r_used",
        ):
            S[name] = block_sem(name)
        x_in = [S[f"x_in{c}"] for c in range(4)]
        strip_in = [S[f"strip_in{c}"] for c in range(RING)]
        low_out = [S["low_out0"], S["low_out1"]]
        panel_in = [S["panel_in0"], S["panel_in1"]]
        slb_in = [S["slb_in0"], S["slb_in1"]]
        x1r_in = [S["x1r_in0"], S["x1r_in1"]]
        out_sent = [S["out_sent0"], S["out_sent1"]]
        N_WTS = 13

        sum_bank = lambda g, dh: 2 * (g % NG2) + dh
        BU, BZ, BT, BG, BH = lambda t: t % 2, 2, 3, lambda t: 4 + t % 2, lambda t: 6 + t % 2
        PA = lambda t: ps[:, t % 4, :]
        PB = lambda t: ps[:, 4 + t % 2, :]
        PC = lambda t: ps[:, 6 + t % 2, :]
        x_view = x.rearrange("(t p) d -> p t d", p=P)
        def gate(eng, sem, value, passed):
            eng.wait_ge(sem, value)
            eng.sem_inc(S[passed], 1)

        block = ctx.enter_context(nc.Block())

        @block.sync
        def _(sp):
            for c in range(4):
                sp.dma_start(xs[:, 8 * c:8 * c + 8, :], x_view[:, 8 * c:8 * c + 8, :]).then_inc(x_in[c], 16)
            for i in range(2 * T):
                half, jb = i // T, i % T
                if i >= RING:
                    old = i - RING
                    sp.wait_ge(S["lo_cast"] if old < T else S["hi_cast"], old % T + 1)
                sp.dma_start(strip[:, i % RING, :], adj[jb * P:(jb + 1) * P, half * (N // 2):(half + 1) * (N // 2)]
                             ).then_inc(strip_in[i % RING], 16)
            sp.wait_ge(S["hi_cast"], T)
            for k in range(LOWP):
                sp.dma_start(a8d[LOWP + k], res[:, k].bitcast(U8)).then_inc(S["res_out"], 16)
            for t in range(T):
                sp.wait_ge(S["x1_ready"], t + 1)
                sp.dma_start(x1d[t * P:(t + 1) * P, :], xs[:, t, :]).then_inc(S["x1_out"], 16)
                if t == T // 2:
                    sp.wait_ge(S["strip_used"], 2 * T)
                    sp.wait_ge(S["res_out"], 16 * LOWP)
                    for k in range(2):
                        sp.wait_ge(low_out[k], 16 * T // 4)
                    for k in range(2):
                        sp.dma_start(pan[:, k].bitcast(U8), a8d[k]).then_inc(panel_in[k], 16)
            sp.wait_ge(S["slrow_ready"], 1)
            sp.dma_start(sld.rearrange("(t p) -> t p", p=P), slrow[:]).then_inc(S["sl_out"], 16)
            sp.wait_ge(S["x1_out"], 16 * T)
            for t in range(2):
                sp.dma_start(x1r[:, t, :], x1d[t * P:(t + 1) * P, :]).then_inc(x1r_in[t], 16)
            sp.wait_ge(S["sl_out"], 16)
            for s in range(2):
                sp.dma_start(slb[:, s, :], sld[s * PW:(s + 1) * PW].partition_broadcast(P)).then_inc(slb_in[s], 16)

            def sp_panel(s, slot):
                gate(sp, S["mask_ready"], s * T + T, "passed_sp")
                gate(sp, S["a_done"], s * 2 + 2, "passed_sp")
                sp.dma_start(pan[:, slot].bitcast(U8), a8d[s + 2]).then_inc(panel_in[slot], 16)
                sp.dma_start(slb[:, slot, :], sld[bass.ds(s * PW + 2 * PW, PW)].partition_broadcast(P)
                             ).then_inc(slb_in[slot], 16)

            def sp_rows(s, last):
                for e in range(2):
                    gate(sp, S["out_ready"], s * 2 + e + 1, "passed_sp")
                    sp.dma_start(out[bass.ds(s * PW + e * P, P), :], ot[:, e, :]).then_inc(out_sent[e], 16)
                    if not last:
                        gate(sp, S["x1r_used"], s * 2 + e + 1, "passed_sp")
                        sp.dma_start(x1r[:, e, :], x1d[bass.ds(s * PW + PW + e * P, P), :]).then_inc(x1r_in[e], 16)

            with sp.Fori(0, NPAN // 2 - 1) as k:
                for m in range(2):
                    sp_panel(k * 2 + m, m)
                    sp_rows(k * 2 + m, False)
            sp_rows(NPAN - 2, False)
            sp_rows(NPAN - 1, True)
            for e in range(2):
                sp.wait_ge(out_sent[e], 16 * NPAN)

        @block.gpsimd
        def _(pool):
            pool.memset(ident[:], 0.0).then_inc(S["pool_step"], 1)
            pool.wait_ge(S["pool_step"], 1)
            pool.affine_select(out=ident[:], in_=ident[:], compare_op=ALU.not_equal, fill=1.0, base=0,
                               pattern=[[-1, P]], channel_multiplier=1).then_inc(S["const_ready"], 1)
            pool.wait_ge(S["const_ready"], 2)
            pool.wait_ge(S["wnorm_ready"], 1)
            pool.tensor_tensor(sc[:, WN], sc[:, WMX], sc[:, MH], ALU.pow).then_inc(S["alpha_pow"], 1)
            pool.wait_ge(S["xmax_part"], 1)
            pool.partition_all_reduce(sc[:, XALL], sc[:, XMX], P, RMAX).then_inc(S["xmax_all"], 1)
            for t in range(T):
                pool.wait_ge(S["stat_ready"], t + 1)
                pool.tensor_tensor(lnst[:, t % 2, 9:10], lnst[:, t % 2, 8:9], sc[:, MH], ALU.pow
                                   ).then_inc(S["rstd_ready"], 1)
            pool.wait_ge(S["nsr_max"], 1)
            pool.partition_all_reduce(sc[:, NMAX], sc[:, NM], P, RMAX).then_inc(S["nmax_ready"], 1)

            def pool_rstd(t, e):
                gate(pool, S["ystat_ready"], t + 1, "passed_pool")
                pool.tensor_tensor(sc1[:, e, RS], sc1[:, e, VE], sc[:, MH], ALU.pow
                                   ).then_inc(S["yrstd_ready"], 1)

            with pool.Fori(0, T // 2) as k:
                for e in range(2):
                    pool_rstd(k * 2 + e, e)

        @block.scalar
        def _(act):
            def low_store(pair):
                act.wait_ge(S["lo_cast"], 2 * pair + 2)
                act.dma_start(a8d[0:LOWP, :, 2 * pair:2 * pair + 2, :].rearrange("k p j i -> p k (j i)"),
                              low[:, pair % 2].rearrange("p k j i -> p k (j i)").bitcast(U8)
                              ).then_inc(low_out[pair % 2], 16)

            kp = lambda a, c: a.rearrange("o (s k p) -> s p (o k)", s=2, p=P)[c]
            act.dma_start(wp[:, :, 0:D], Wg.rearrange("(k p) d -> p k d", p=P)).then_inc(S["wts_in"], 16)
            act.dma_start(wp[:, :, WG:WC], Wsa.rearrange("(k p) d -> p k d", p=P)).then_inc(S["wts_in"], 16)
            with nc.allow_non_contiguous_dma(reason="256 weights, one column each"):
                for c, (a, s) in enumerate(((Wa, 0), (Wb, 0), (Wa, 1), (Wb, 1))):
                    act.dma_start(wp[:, :, D + c], kp(a, s)).then_inc(S["wts_in"], 16)
            act.dma_start(asab[:], asa.rearrange("o d -> (o d)").partition_broadcast(P)).then_inc(S["wts_in"], 16)
            act.dma_start(w0[:], W0.rearrange("(k p) d -> p k d", p=P)).then_inc(S["wts_in"], 16)
            act.dma_start(b0b[:], b0.partition_broadcast(P)).then_inc(S["wts_in"], 16)
            act.dma_start(bgb[:], bg.partition_broadcast(P)).then_inc(S["wts_in"], 16)
            act.dma_start(sc[:, 14:15], ba.partition_broadcast(P)).then_inc(S["wts_in"], 16)
            act.dma_start(sc[:, 15:16], bb.partition_broadcast(P)).then_inc(S["wts_in"], 16)

            act.wait_ge(S["sx_ready"], 1)
            for jb in range(T):
                act.activation(y[:, jb, 0, :], xs[:, jb, :], ACT.Copy, scale=sc[:, SX]).then_inc(S["yhi_ready"], 1)
                if jb % 4 == 3:
                    low_store(jb // 4)
            for pair in range(T // 4, T // 2):
                low_store(pair)

            def evac(half):
                act.wait_ge(S["strip_used"], T * (half + 1))
                for dh in range(KD):
                    for g in (NG2 * half, NG2 * half + 2):
                        act.copy(acct[g][:, dh, :], ps[:, sum_bank(g, dh), :]).then_inc(S["evac_act"], 1)

            evac(0)
            for jb in range(T):
                i = T + jb
                act.wait_ge(strip_in[i % RING], 16 * (i // RING + 1))
                act.activation(res[:, :, jb, :], strip[:, i % RING, :].rearrange("p (k i) -> p k i", i=PW),
                               ACT.Copy, accum_out=dega[:, jb:jb + 1], saturate=False).then_inc(S["hi_cast"], 1)
            evac(1)

            def z_scale(t):
                if t >= 2:
                    act.wait_ge(S["zt_done"], t - 1)
                act.activation(zx[:, t % 2, :], xs[:, t, :], ACT.Copy, scale=zs[:, t:t + 1]).then_inc(S["zx_ready"], 1)

            def x1t_copy(t):
                act.wait_ge(S["x1t_done"], t + 1)
                act.copy(x1t[:, t % 2].rearrange("p k i -> p (k i)"), ps[:, BT, 0:D]
                         ).then_inc(S["x1t_ready"], 1)

            def proj_copies(t):
                act.wait_ge(S["proj_done"], t + 1)
                act.copy(ex[:, t, :], ps[:, BG(t), GC:WG])
                act.activation(fa[:, t, 0, :], ps[:, BG(t), 0:GC], ACT.Copy, scale=sc[:, AL]
                               ).then_inc(S["ghi_ready"], 1)
                act.copy(h[:, t, :], ps[:, BH(t), 0:D]).then_inc(S["h_ready"], 1)

            act.wait_ge(S["scale_ready"], 1)
            act.wait_ge(S["qa_ready"], 1)
            for c in range(2):
                act.wait_ge(low_out[c], 16 * T // 4)
            z_scale(0)
            for n in range(T + 2):
                if n < T - 1:
                    z_scale(n + 1)
                if n >= 2:
                    proj_copies(n - 2)
                if 1 <= n <= T:
                    x1t_copy(n - 1)
            act.wait_ge(S["slt_done"], 1)
            act.wait_ge(S["res_out"], 16 * LOWP)
            act.copy(slrow[:], ps[0:T, BU(0), 0:P]).then_inc(S["slrow_ready"], 1)
            act.wait_ge(S["arg_ready"], 1)
            act.activation(q[:], tq[:], ACT.Exp)
            act.activation(qp[:], tq[:], ACT.Exp, scale=0.01)
            act.activation(pp[:, :, 0], tpc[:], ACT.Exp)
            act.activation(pp[:, :, 1], tp[:], ACT.Exp, scale=0.01).then_inc(S["pq_ready"], 1)
            act.wait_ge(S["qa_ready"], 2)
            act.wait_ge(S["x1_out"], 16 * T)
            for t in range(T):
                act.activation(fb[:, t, 0, 0:D], h[:, t, :], ACT.Copy, scale=qa[:, t:t + 1]
                               ).then_inc(S["fbhi_ready"], 1)
                if t % 2 == 0:
                    act.activation(fc[:, t, 0, 0:D], h[:, t, :], ACT.Copy, scale=qpa[:, t:t + 1]
                                   ).then_inc(S["fchi_ready"], 1)

            def act_tile(t, e):
                gate(act, S["a_done"], t + 1, "passed_act")
                for c in range(2):
                    act.activation(sc1[:, e, 10 + c:11 + c], PA(t_mod4[0])[:, D + c:D + c + 1], ACT.Sigmoid,
                                   scale=sc[:, INVA], bias=rab[:, bass.ds(t, 1), c]).then_inc(S["att_ready"], 1)
                gate(act, S["att_ready"], t * 2 + 2, "passed_act")
                gate(act, S["w_ready"], t + 1, "passed_act")
                act.activation(wb[:, e, :], w[:, e, :], ACT.Copy, scale=sc1[:, e, 11:12]).then_inc(S["wb_ready"], 1)
                gate(act, S["epi_read"], t + 1, "passed_act")
                act.activation(sg[:, e, :], w[:, e, :], ACT.Sigmoid).then_inc(S["sg_ready"], 1)

            t_mod4 = [0]
            with act.Fori(0, T // 4) as k:
                for m in range(4):
                    t_mod4[0] = m
                    act_tile(k * 4 + m, m % 2)

        @block.vector
        def _(dve):
            st = Steps(dve, S["dve_step"])
            dve.memset(sc[:, MH], -0.5)
            dve.memset(ones[:], 1.0)
            dve.memset(sc[:, ONE], 1.0).then_inc(S["const_ready"], 1)
            dve.wait_ge(S["wts_in"], 16 * 12)
            for k in range(KD):
                for c in range(2):
                    st.then(dve.scalar_tensor_tensor(out=wtmp[:], in0=wp[:, k, WG:WC], scalar=1.0,
                                                     in1=asab[:, c * D:(c + 1) * D], op0=ALU.mult, op1=ALU.mult,
                                                     accum_out=wp[:, k, GC + 2 + c:GC + 3 + c]))
                    st.sync()
            dve.tensor_tensor(wsq[:].rearrange("p k c -> p (k c)"), wp[:].rearrange("p k c -> p (k c)"),
                              wp[:].rearrange("p k c -> p (k c)"), ALU.mult).then_inc(S["wsq_ready"], 1)
            dve.wait_ge(S["wsum_ready"], 1)
            st.then(dve.tensor_reduce(sc[:, 16:17], ps[:, 0, 0:WC - WG], AX, ALU.max))
            st.then(dve.tensor_reduce(sc[:, 17:18], ps[:, 1, 0:WG], AX, ALU.max))
            st.sync()
            st.then(dve.tensor_tensor(sc[:, WMX], sc[:, 16:17], sc[:, 17:18], ALU.max))
            st.sync()
            dve.tensor_scalar(sc[:, WMX], sc[:, WMX], 1e-30, None, ALU.max).then_inc(S["wnorm_ready"], 1)
            for c in range(4):
                dve.wait_ge(x_in[c], 16)
                st.then(dve.tensor_reduce(sc[:, c:c + 1], xs[:, 8 * c:8 * c + 8, :].rearrange("p t d -> p (t d)"),
                                          AX, ALU.max, apply_absolute_value=True))
            st.sync()
            dve.tensor_reduce(sc[:, XMX], sc[:, XM], AX, ALU.max).then_inc(S["xmax_part"], 1)
            dve.wait_ge(S["alpha_pow"], 1)
            st.then(dve.tensor_scalar(sc[:, AL], sc[:, WN], F16_TOP / D ** 0.5, None, ALU.mult))
            st.sync()
            dve.reciprocal(sc[:, INVA], sc[:, AL]).then_inc(S["qa_ready"], 1)
            dve.wait_ge(S["xmax_all"], 1)
            st.then(dve.tensor_scalar(sc[:, XG], sc[:, XALL], 1e-30, 1.0 / F16_TOP, ALU.max, ALU.mult))
            st.sync()
            st.then(dve.tensor_copy(sc[:, ISX], sc[:, XG]))
            dve.reciprocal(sc[:, SX], sc[:, XG]).then_inc(S["sx_ready"], 1)

            for jb in range(T):
                pair, jj = jb // 2, jb % 2
                if jb >= 1 or True:
                    dve.wait_ge(strip_in[jb % RING], 16 * (jb // RING + 1))
                if pair >= 2 and jj == 0:
                    dve.wait_ge(low_out[pair % 2], 16 * (pair // 2))
                    dve.wait_ge(S["strip_used"], 2 * pair - 2)
                dve.tensor_scalar(out=low[:, pair % 2, :, jj, :],
                                  in0=strip[:, jb % RING, :].rearrange("p (k i) -> p k i", i=PW),
                                  scalar1=0.0, scalar2=0.0, op0=ALU.add, op1=ALU.add,
                                  accum_out=degv[:, jb:jb + 1], saturate=False).then_inc(S["lo_cast"], 1)
                dve.wait_ge(S["yhi_ready"], jb + 1)
                dve.scalar_tensor_tensor(out=y[:, jb, 1, :], in0=xs[:, jb, :], scalar=sc[:, SX],
                                         in1=y[:, jb, 0, :], op0=ALU.mult, op1=ALU.subtract
                                         ).then_inc(S["ylo_ready"], 1)

            def evac(half):
                dve.wait_ge(S["strip_used"], T * (half + 1))
                for dh in range(KD):
                    for g in (NG2 * half + 1, NG2 * half + 3):
                        dve.tensor_copy(acct[g][:, dh, :], ps[:, sum_bank(g, dh), :]).then_inc(S["evac_dve"], 1)

            evac(0)
            dve.wait_ge(S["hi_cast"], T)
            dve.wait_ge(S["lo_cast"], T)
            st.then(dve.tensor_tensor(deg[:], degv[:], dega[:], ALU.add))
            st.sync()
            st.then(dve.tensor_scalar(deg[:], deg[:], 1.0, None, ALU.max))
            st.sync()
            st.then(dve.tensor_scalar(zs[:], deg[:], 1.0, sc[:, SX], ALU.add, ALU.mult))
            st.then(dve.reciprocal(us[:], deg[:]))
            st.sync()
            dve.tensor_scalar(us[:], us[:], sc[:, ISX], None, ALU.mult).then_inc(S["scale_ready"], 1)
            dve.wait_ge(S["scale_ready"], 1)
            evac(1)

            def add_share(t):
                g, tt = t // TG, t % TG
                a = acct[g][:, :, tt * P:(tt + 1) * P]
                dve.wait_ge(S["evac_act"], 8 if g >= NG2 else 4)
                dve.wait_ge(S["evac_dve"], 8 if g >= NG2 else 4)
                dve.wait_ge(S["zt_done"], t + 1)
                dve.tensor_tensor(a, a, ps[:, BZ, 0:D].rearrange("p (k i) -> p k i", k=KD), ALU.add
                                  ).then_inc(S["acct_ready"], 1)

            def g_lo(t):
                dve.wait_ge(S["ghi_ready"], t + 1)
                dve.scalar_tensor_tensor(out=fa[:, t, 1, :], in0=ps[:, BG(t), 0:GC], scalar=sc[:, AL],
                                         in1=fa[:, t, 0, :], op0=ALU.mult, op1=ALU.subtract
                                         ).then_inc(S["glo_ready"], 1)

            add_share(0)
            for n in range(T):
                e = n % 2
                u = ps[:, BU(n), 0:D]
                ln = lnst[:, e, :]
                dve.wait_ge(S["u_done"], n + 1)
                st.then(dve.scalar_tensor_tensor(out=u, in0=u, scalar=us[:, n:n + 1], in1=b0b[:], op0=ALU.mult,
                                                 op1=ALU.add))
                st.sync()
                dve.scalar_tensor_tensor(out=xs[:, n, :], in0=u, scalar=0.0, in1=xs[:, n, :], op0=ALU.max,
                                         op1=ALU.add).then_inc(S["r2_done"], 1)
                dve.wait_ge(S["r2_done"], n + 1)
                st.then(dve.bn_stats(ln[:, BN], xs[:, n, :]))
                st.sync()
                st.then(dve.bn_aggr(ln[:, MV], ln[:, BN]))
                st.sync()
                dve.tensor_scalar(ln[:, VE], ln[:, 7:8], EPS, None, ALU.add).then_inc(S["stat_ready"], 1)
                if n < T - 1:
                    add_share(n + 1)
                dve.wait_ge(S["rstd_ready"], n + 1)
                dve.tensor_scalar(xs[:, n, :], xs[:, n, :], ln[:, 6:7], ln[:, RS], ALU.subtract, ALU.mult
                                  ).then_inc(S["x1_ready"], 1)
                if n >= 2:
                    g_lo(n - 2)
            g_lo(T - 2)
            g_lo(T - 1)

            dve.wait_ge(S["h_ready"], T)
            dve.wait_ge(S["u_done"], T)
            dve.wait_ge(S["res_out"], 16 * LOWP)
            dve.tensor_copy(slc[:], ex[:, :, 2]).then_inc(S["sl_ready"], 1)
            st.then(dve.tensor_scalar(nsr[:], ex[:, :, 3], -1.0, None, ALU.mult))
            st.sync()
            dve.tensor_reduce(sc[:, NM], nsr[:], AX, ALU.max).then_inc(S["nsr_max"], 1)
            for c in range(2):
                st.then(dve.tensor_scalar(rab[:, :, c], ex[:, :, c], sc[:, 14 + c:15 + c], None, ALU.add))
            dve.wait_ge(S["nmax_ready"], 1)
            dve.wait_ge(S["sl_ready"], 1)
            st.then(dve.tensor_scalar(tq[:], nsr[:], sc[:, NMAX], None, ALU.subtract))
            st.then(dve.tensor_scalar(tp[:], slc[:], -1.0, sc[:, NMAX], ALU.mult, ALU.add))
            st.sync()
            dve.tensor_scalar(tpc[:], tp[:], P_TOP, None, ALU.min).then_inc(S["arg_ready"], 1)
            dve.wait_ge(S["pq_ready"], 1)
            st.then(dve.tensor_scalar(qa[:], q[:], sc[:, AL], None, ALU.mult))
            dve.tensor_scalar(qpa[:], qp[:], sc[:, AL], None, ALU.mult).then_inc(S["qa_ready"], 1)
            dve.wait_ge(S["x1_out"], 16 * T)
            dve.wait_ge(S["qa_ready"], 2)
            for f, v in ((fb, q), (fc, qp)):
                st.then(dve.tensor_scalar(f[:, :, 0, D], v[:], KAPPA, None, ALU.mult))
                st.sync()
                st.then(dve.scalar_tensor_tensor(out=f[:, :, 1, D], in0=v[:], scalar=KAPPA, in1=f[:, :, 0, D],
                                                 op0=ALU.mult, op1=ALU.subtract))
            for t in range(T):
                if t % 2 == 1:
                    st.then(dve.tensor_scalar(fc[:, t, 0, 0:D], h[:, t, :], qpa[:, t:t + 1], None, ALU.mult))
                dve.wait_ge(S["fbhi_ready"], t + 1)
                dve.scalar_tensor_tensor(out=fb[:, t, 1, 0:D], in0=h[:, t, :], scalar=qa[:, t:t + 1],
                                         in1=fb[:, t, 0, 0:D], op0=ALU.mult, op1=ALU.subtract)
                if t % 2 == 0:
                    dve.wait_ge(S["fchi_ready"], t // 2 + 1)
                else:
                    st.sync()
                dve.scalar_tensor_tensor(out=fc[:, t, 1, 0:D], in0=h[:, t, :], scalar=qpa[:, t:t + 1],
                                         in1=fc[:, t, 0, 0:D], op0=ALU.mult, op1=ALU.subtract
                                         ).then_inc(S["feat_ready"], 1)
            dve.wait_ge(S["feat_ready"], T)

            def masks(slot, lo, hi):
                for jb in range(lo, hi):
                    dve.scalar_tensor_tensor(out=bm[:, slot, jb, :], in0=slb[:, slot, :], scalar=nsr[:, jb:jb + 1],
                                             in1=pan[:, slot, jb, :], op0=ALU.is_ge, op1=ALU.mult, saturate=False)
                    dve.scalar_tensor_tensor(out=cm[:, slot, jb, :], in0=slb[:, slot, :], scalar=nsr[:, jb:jb + 1],
                                             in1=pan[:, slot, jb, :], op0=ALU.is_lt, op1=ALU.mult, saturate=False
                                             ).then_inc(S["mask_ready"], 1)

            def masks_waits(s, slot, nth):
                gate(dve, panel_in[slot], nth * 16, "passed_dve")
                gate(dve, slb_in[slot], nth * 16, "passed_dve")

            def epilogue(t, m):
                e = m % 2
                s1 = sc1[:, e, :]
                gate(dve, S["bc_done"], t + 1, "passed_dve")
                ppt = lambda a, b: pp[:, bass.ds(t, 1), a:b].rearrange("p o c -> p (o c)")
                gate(dve, S["att_ready"], t * 2 + 2, "passed_dve")
                dve.scalar_tensor_tensor(out=w[:, e, :], in0=PA(m)[:, 0:D], scalar=sc[:, INVA], in1=bgb[:],
                                         op0=ALU.mult, op1=ALU.add).then_inc(S["w_ready"], 1)
                st.then(dve.tensor_scalar(s1[:, D1], PC(m)[:, D:D + 1], ppt(1, 2), None, ALU.mult))
                st.sync()
                st.then(dve.scalar_tensor_tensor(out=s1[:, DD], in0=PB(m)[:, D:D + 1], scalar=ppt(0, 1),
                                                 in1=s1[:, D1], op0=ALU.mult, op1=ALU.add))
                st.sync()
                st.then(dve.tensor_scalar(s1[:, D2], s1[:, DD], 1.0 / KAPPA, EPS, ALU.mult, ALU.add))
                st.sync()
                st.then(dve.reciprocal(s1[:, REC], s1[:, D2]))
                st.then(dve.tensor_scalar(s1[:, CI], s1[:, 10:11], sc[:, INVA], None, ALU.mult))
                st.sync()
                st.then(dve.tensor_scalar(s1[:, CBC], ppt(0, 2), s1[:, REC], s1[:, CI], ALU.mult, ALU.mult))
                st.sync()
                gate(dve, S["wb_ready"], t + 1, "passed_dve")
                st.then(dve.scalar_tensor_tensor(out=wb[:, e, :], in0=PB(m)[:, 0:D], scalar=s1[:, 17:18],
                                                 in1=wb[:, e, :], op0=ALU.mult, op1=ALU.add))
                st.sync()
                dve.scalar_tensor_tensor(out=w[:, e, :], in0=PC(m)[:, 0:D], scalar=s1[:, 18:19],
                                         in1=wb[:, e, :], op0=ALU.mult, op1=ALU.add).then_inc(S["epi_read"], 1)
                gate(dve, S["sg_ready"], t + 1, "passed_dve")
                nth = t_half(t, m)
                gate(dve, x1r_in[e], nth * 16, "passed_dve")
                dve.tensor_tensor(sg[:, e, :], sg[:, e, :], x1r[:, e, :], ALU.add).then_inc(S["x1r_used"], 1)
                gate(dve, S["x1r_used"], t + 1, "passed_dve")
                st.then(dve.bn_stats(s1[:, BN], sg[:, e, :]))
                gate(dve, S["dve_step"], st.n + st.base, "passed_dve")
                st.then(dve.bn_aggr(s1[:, MV], s1[:, BN]))
                st.sync()
                dve.tensor_scalar(s1[:, VE], s1[:, 7:8], EPS, None, ALU.add).then_inc(S["ystat_ready"], 1)
                gate(dve, S["yrstd_ready"], t + 1, "passed_dve")
                if first[0] and m < 2:
                    pass
                else:
                    gate(dve, out_sent[e], nth * 16 - 16, "passed_dve")
                dve.tensor_scalar(ot[:, e, :], sg[:, e, :], s1[:, 6:7], s1[:, RS], ALU.subtract, ALU.mult
                                  ).then_inc(S["out_ready"], 1)

            first = [True]
            half = [0]

            def t_half(t, m):
                return half[0] + m // 2 + 1

            masks_waits(None, 0, 1)
            masks(0, 0, T)

            def panel_step(s, m, nth, with_masks):
                nslot = 1 - m
                if with_masks:
                    masks_waits(s, nslot, nth)
                    masks(nslot, 0, T // 2)
                epilogue(s * 2, 2 * m)
                if with_masks:
                    masks(nslot, T // 2, T)
                epilogue(s * 2 + 1, 2 * m + 1)

            panel_step(0, 0, 1, True)
            first[0] = False
            panel_step(1, 1, 2, True)
            per = None
            n0 = st.n
            with dve.Fori(1, NPAN // 2 - 1) as k:
                st.n, st.base = n0, k * PER_PAIR - PER_PAIR
                half[0] = k * 2
                panel_step(k * 2, 0, k + 1, True)
                panel_step(k * 2 + 1, 1, k + 2, True)
                per = st.n - n0
            assert per == PER_PAIR, per
            st.n, st.base = n0 + (NPAN // 2 - 2) * per, 0
            half[0] = NPAN - 2
            panel_step(NPAN - 2, 0, NPAN // 2, True)
            panel_step(NPAN - 1, 1, None, False)

        @block.tensor
        def _(pe):
            pe.wait_ge(S["wsq_ready"], 1)
            pe.wait_ge(S["const_ready"], 2)
            for b, (c0, c1) in enumerate(((WG, WC), (0, WG))):
                for k in range(KD):
                    mm = pe.matmul(ps[:, b, 0:c1 - c0], ones[:], wsq[:, k, c0:c1], start=(k == 0), stop=(k == KD - 1))
            mm.then_inc(S["wsum_ready"], 1)
            pe.wait_ge(S["wnorm_ready"], 1)

            for i in range(2 * T):
                half, jb = i // T, i % T
                pe.wait_ge(S["hi_cast" if half else "lo_cast"], jb + 1)
                if not half:
                    pe.wait_ge(S["ylo_ready"], jb + 1)
                for dh in range(KD):
                    for part in range(2):
                        for g in range(NG2):
                            if i == T and part == 0:
                                pe.wait_ge(S["evac_dve" if g % 2 else "evac_act"], 2 * dh + g // 2 + 1)
                            a = res[:, 2 * g:2 * g + 2, jb, :] if half else low[:, jb // 2 % 2, 2 * g:2 * g + 2, jb % 2, :]
                            mm = pe.matmul(ps[:, sum_bank(g, dh), :], y[:, jb, part, dh * P:(dh + 1) * P], a,
                                           start=(jb == 0 and part == 0), stop=(jb == T - 1 and part == 1))
                mm.then_inc(S["strip_used"], 1)

            def z_step(t):
                pe.wait_ge(S["zx_ready"], t + 1)
                if t >= 1:
                    pe.wait_ge(S["acct_ready"], t)
                else:
                    pe.wait_ge(S["evac_dve"], 5)
                for k in range(KD):
                    mm = pe.transpose(ps[:, BZ, k * P:(k + 1) * P], zx[:, t % 2, k * P:(k + 1) * P], ident[:])
                mm.then_inc(S["zt_done"], 1)

            def u_step(t):
                g, tt = t // TG, t % TG
                pe.wait_ge(S["acct_ready"], t + 1)
                if t < 2:
                    pe.wait_ge(S["evac_act"], 7)
                else:
                    pe.wait_ge(S["r2_done"], t - 1)
                for k in range(KD):
                    mm = pe.matmul(ps[:, BU(t), 0:D], acct[g][:, k, tt * P:(tt + 1) * P],
                                   w0[:, k, :], start=(k == 0), stop=(k == KD - 1))
                mm.then_inc(S["u_done"], 1)

            def t_step(t):
                pe.wait_ge(S["x1_ready"], t + 1)
                if t >= 1:
                    pe.wait_ge(S["x1t_ready"], t)
                else:
                    pe.wait_ge(S["evac_dve"], 7)
                for k in range(KD):
                    mm = pe.transpose(ps[:, BT, k * P:(k + 1) * P], xs[:, t, k * P:(k + 1) * P], ident[:])
                mm.then_inc(S["x1t_done"], 1)

            def p_step(t):
                pe.wait_ge(S["x1t_ready"], t + 1)
                if t < 2:
                    pe.wait_ge(S["evac_act"], 8)
                    pe.wait_ge(S["evac_dve"], 8)
                else:
                    pe.wait_ge(S["h_ready"], t - 1)
                    pe.wait_ge(S["glo_ready"], t - 1)
                for b, c0, c1 in ((BG(t), 0, WG), (BH(t), WG, WC)):
                    for k in range(KD):
                        mm = pe.matmul(ps[:, b, 0:c1 - c0], x1t[:, t % 2, k, :], wp[:, k, c0:c1],
                                       start=(k == 0), stop=(k == KD - 1))
                mm.then_inc(S["proj_done"], 1)

            z_step(0)
            for n in range(T + 2):
                if n < T:
                    u_step(n)
                if n < T - 1:
                    z_step(n + 1)
                if n >= 2:
                    p_step(n - 2)
                if 1 <= n <= T:
                    t_step(n - 1)

            pe.wait_ge(S["sl_ready"], 1)
            pe.transpose(ps[0:T, BU(0), 0:P], slc[:], ident[:]).then_inc(S["slt_done"], 1)

            def a_tile(t, m, slot):
                for jb in range(T):
                    for part in range(2):
                        mm = pe.matmul(PA(m)[:, 0:GC], pan[:, slot, jb, (m % 2) * P:(m % 2 + 1) * P],
                                       fa[:, jb, part, :], start=(jb == 0 and part == 0),
                                       stop=(jb == T - 1 and part == 1))
                mm.then_inc(S["a_done"], 1)

            def bc_tile(m, slot, chase):
                for jb in range(T):
                    if chase:
                        pe.wait_ge(S["mask_ready"], jb + 1)
                    for out_, mask, f in ((PB(m), bm, fb), (PC(m), cm, fc)):
                        for part in range(2):
                            mm = pe.matmul(out_[:, 0:HC], mask[:, slot, jb, (m % 2) * P:(m % 2 + 1) * P],
                                           f[:, jb, part, :], start=(jb == 0 and part == 0),
                                           stop=(jb == T - 1 and part == 1))
                mm.then_inc(S["bc_done"], 1)

            pe.wait_ge(S["glo_ready"], T)
            pe.wait_ge(S["slrow_ready"], 1)
            pe.wait_ge(S["h_ready"], T)
            for t in range(4):
                if t % 2 == 0:
                    pe.wait_ge(panel_in[t // 2], 16)
                a_tile(t, t, t // 2)

            def panel(s, m, more, chase, nth):
                for e in range(2):
                    if not chase:
                        gate(pe, S["mask_ready"], s * T + T, "passed_pe")
                        gate(pe, S["epi_read"], s * 2 + e - 1, "passed_pe")
                    bc_tile(2 * m + e, m, chase and e == 0)
                if more:
                    gate(pe, panel_in[m], nth * 16, "passed_pe")
                    for e in range(2):
                        gate(pe, S["epi_read"], s * 2 + e + 1, "passed_pe")
                        a_tile(None, 2 * m + e, m)

            panel(0, 0, True, True, 2)
            panel(1, 1, True, False, 2)
            with pe.Fori(1, NPAN // 2 - 1) as k:
                panel(k * 2, 0, True, False, k + 2)
                panel(k * 2 + 1, 1, True, False, k + 2)
            panel(NPAN - 2, 0, False, False, None)
            panel(NPAN - 1, 1, False, False, None)


PER_PAIR = 4 * 9


_INS = ['x', 'adj', 'L0_gnn_W', 'L0_gnn_b', 'L1_gnn_W_sa', 'L1_gnn_a_sa', 'L1_gnn_W_gcnb', 'L1_gnn_b_gcnb',
        'L1_gnn_Wa', 'L1_gnn_ba', 'L1_gnn_Wb', 'L1_gnn_bb']


def kernel(**inputs):
    import numpy as _np
    import concourse.bacc as _bacc
    from concourse import mybir as _mybir
    from concourse.bass_utils import run_bass_kernel_spmd as _run

    nc = _bacc.Bacc("TRN2", target_bir_lowering=False, num_devices=1)
    arrays, args = {}, []
    for name in _INS:
        a = _np.ascontiguousarray(inputs[name])
        arrays[f"in_{name}_dram"] = a
        args.append(nc.dram_tensor(f"in_{name}_dram", a.shape, _mybir.dt.from_np(a.dtype), kind="ExternalInput").ap())
    o = nc.dram_tensor("out_0_dram", (N, D), _mybir.dt.float32, kind="ExternalOutput").ap()
    build(nc, *args, o)
    r = _run(nc, [arrays], core_ids=[0])
    return r.results[0]["out_0_dram"]
```

```python
from contextlib import ExitStack

import numpy as np
import concourse.bass as bass
from concourse import mybir

ALU = mybir.AluOpType
ACT = mybir.ActivationFunctionType
AX = mybir.AxisListType.X
F32, F16, F8 = mybir.dt.float32, mybir.dt.float16, mybir.dt.float8e4
U8, U32 = mybir.dt.uint8, mybir.dt.uint32
RMAX = bass.bass_isa.ReduceOp.max
RADD = bass.bass_isa.ReduceOp.add

P = 128
N = 4096
D = 256
T = N // P
KD = D // P
PW = 256
NPAN = N // PW
LOWP = NPAN // 2
GW = 512
TG = GW // P
NG = N // GW
NG2 = NG // 2
RING = 4
CH = 8
NCH = T // CH
GC = D + 2
HC = D + 1
NEX = 4
WG = GC + NEX
WC = WG + D
EPS = 1e-5
F16_TOP = 32768.0
KAPPA = 16384.0
MU = 16384.0
SLOPE = 0.01
EDGE, NONE = 8, 128
EDGE_VAL = 2.0 ** -6
XCUT = (0, 8, 16, 24, 28, 30, 32)
LR = 4
ER = 4

BASE = 16512
O_FA = 0
O_FB = O_FA + T * 2 * GC * 2
O_X = O_FB + T * 2 * HC * 2
O_HB = O_X + T * D * 4
O_RES = O_HB + T * D * 4
O_PERS = O_RES + T * N // 2
TOP = 229344 - BASE


class Steps:

    def __init__(self, eng, sem):
        self.eng, self.sem, self.n, self.base = eng, sem, 0, 0

    def then(self, ins):
        ins.then_inc(self.sem, 1)
        self.n += 1

    def sync(self):
        self.eng.wait_ge(self.sem, self.n + self.base)


def build(nc, x, adj, W0, b0, Wsa, asa, Wg, bg, Wa, ba, Wb, bb, out):
    def at(name, shape, dt, off):
        size = int(np.prod(shape[1:])) * mybir.dt.size(dt)
        assert off + size <= TOP, (name, off + size, TOP)
        return nc.alloc_sbuf_tensor_at(name, shape, dt, offset=BASE + off)

    class Area:

        def __init__(self, off, end):
            self.off, self.end = off, end

        def __call__(self, name, shape, dt):
            t = at(name, shape, dt, self.off)
            self.off += -(-int(np.prod(shape[1:])) * mybir.dt.size(dt) // 32) * 32
            assert self.off <= self.end, (name, self.off, self.end)
            return t

    fa = at("fa", [P, T, 2, GC], F16, O_FA)
    fb = at("fb", [P, T, 2, HC], F16, O_FB)
    y = at("y", [P, T, 2, D], F16, O_FB)
    xs = at("xs", [P, T, D], F32, O_X)
    strip = at("strip", [P, RING, N // 2], F32, O_HB)
    h = at("h", [P, T, D], F32, O_HB)
    em = at("em", [P, 2, 2, T, PW], F16, O_X)
    res = at("res", [P, LOWP, T, PW], U8, O_RES)
    low = at("low", [P, LR, LOWP, 2, PW], U8, O_FA)
    area = Area(O_FA, O_FA + LR * LOWP * 2 * PW)
    wsq = area("wsq", [P, KD, WC], F32)
    asab = area("asab", [P, 2 * D], F32)
    wsum = area("wsum", [P, WC], F32)
    O_ACCT = O_FA + LR * LOWP * 2 * PW
    acct = [at(f"acct{g}", [P, KD, GW], F32, O_ACCT + g * KD * GW * 4) for g in range(NG2)]
    area = Area(O_FB, O_X)
    acct += [area(f"acct{g}", [P, KD, GW], F32) for g in range(NG2, NG)]
    x1t = area("x1t", [P, 2, KD, P], F32)
    lnst = area("lnst", [P, 2, 12], F32)
    pan = at("pan", [P, 2, T, PW], U8, O_RES)
    ec = at("ec", [P, ER, CH, PW], F32, O_RES + 4 * T * PW)
    area = Area(O_RES + 2 * T * PW, O_RES + 4 * T * PW)
    slb = area("slb", [P, 2, PW], F32)
    x1r = area("x1r", [P, 2, D], F32)
    w = area("w", [P, 2, D], F32)
    wb = area("wb", [P, 2, D], F32)
    sg = area("sg", [P, 2, D], F32)
    ot = area("ot", [P, 2, D], F32)
    nsr = area("nsr", [P, T], F32)
    slc = area("slc", [P, T], F32)
    sr8 = area("sr8", [P, T], F32)
    tq = area("tq", [P, T], F32)
    ta = area("ta", [P, T], F32)
    tb = area("tb", [P, T], F32)
    q = area("q", [P, T], F32)
    qa = area("qa", [P, T], F32)
    rr = area("rr", [P, T], F32)
    rden = area("rden", [P, T], F32)
    rnum = area("rnum", [P, T], F32)
    rab = area("rab", [P, T, 2], F32)
    slrow = area("slrow", [T, P], F32)
    sc1 = area("sc1", [P, 2, 32], F32)
    area = Area(O_PERS, TOP)
    wp = area("wp", [P, KD, WC], F32)
    w0 = area("w0", [P, KD, D], F32)
    b0b = area("b0b", [P, D], F32)
    bgb = area("bgb", [P, D], F32)
    ident = area("ident", [P, P], F32)
    zx = area("zx", [P, 2, D], F32)
    ex = area("ex", [P, T, NEX], F32)
    degv = area("degv", [P, T], F32)
    dega = area("dega", [P, T], F32)
    deg = area("deg", [P, T], F32)
    zs = area("zs", [P, T], F32)
    us = area("us", [P, T], F32)
    sc = area("sc", [P, 32], F32)
    col = iter(range(32))
    column = lambda n=1: (lambda a: slice(a[0], a[-1] + 1))([next(col) for _ in range(n)])
    XM, SX, ISX, MH, E8, NM, NMAX, XMX, WN, AL, INVA, HINVA, XALL, XG, WMX, TMP, IAL, CNONE, BAB = (
        column(len(XCUT) - 1), *(column() for _ in range(17)), column(2))
    BN, MV, VE, RS, ATT, TH, D2, REC, CE = (
        slice(0, 6), slice(6, 8), slice(8, 9), slice(9, 10), slice(10, 12), slice(12, 14), slice(14, 15),
        slice(15, 16), slice(16, 17))

    a8d = nc.dram_tensor("a8_scratch", [NPAN, P, T, PW], U8)
    x1d = nc.dram_tensor("x1_scratch", [N, D], F32)
    sld = nc.dram_tensor("sl_scratch", [N], F32)

    with ExitStack() as ctx:
        ps = ctx.enter_context(nc.psum_tensor("ps", [P, 8, 512], F32))
        block_sem = lambda name: ctx.enter_context(nc.semaphore(name))
        S = {}
        for name in (
            "x_in0", "x_in1", "x_in2", "x_in3", "x_in4", "x_in5", "wts_in", "wts_ready", "wsq_ready", "wsum_ready", "wnorm_ready",
            "alpha_pow", "const_ready", "b_made", "xmax_part", "xmax_all", "sx_ready", "strip_in0", "strip_in1",
            "strip_in2", "strip_in3", "lo_cast", "hi_cast", "scale_ready", "yhi_ready", "ylo_ready",
            "strip_used", "low_out0", "low_out1", "low_out2", "low_out3", "res_out", "zx_ready", "zt_done", "acct_ready", "evac_act", "evac_dve",
            "u_done", "r2_done", "stat_ready", "rstd_ready", "x1_ready", "x1t_done", "x1t_ready", "proj_done",
            "ghi_ready", "h_ready", "glo_ready", "x1_out", "m_done", "nsr_ready", "nsr_max", "nmax_ready", "arg_ready",
            "pq_ready", "sl_ready", "slt_done", "slrow_ready", "sl_out", "qa_ready", "fbhi_ready", 
            "feat_ready", "panel_in0", "panel_in1", "slb_in0", "slb_in1", "t_ready", "e_ready", "ehi_ready", "elo_ready", "a_done", "bc_done",
            "att_ready", "th_ready", "w_ready", "wb_ready", "epi_read", "sg_ready", "ystat_ready", "yrstd_ready", "out_ready",
            "x1r_in0", "x1r_in1", "out_sent0", "out_sent1", "dve_step", "pool_step", "passed_pe", "passed_dve",
            "passed_act", "passed_sp", "passed_pool", "x1r_used",
        ):
            S[name] = block_sem(name)
        x_in = [S[f"x_in{c}"] for c in range(len(XCUT) - 1)]
        strip_in = [S[f"strip_in{c}"] for c in range(RING)]
        low_out = [S[f"low_out{c}"] for c in range(LR)]
        panel_in = [S["panel_in0"], S["panel_in1"]]
        slb_in = [S["slb_in0"], S["slb_in1"]]
        x1r_in = [S["x1r_in0"], S["x1r_in1"]]
        out_sent = [S["out_sent0"], S["out_sent1"]]

        sum_bank = lambda g, dh: 2 * (g % NG2) + dh
        BU, BZ, BT, BG, BH = lambda t: t % 2, 2, 3, lambda t: 4 + t % 2, lambda t: 6 + t % 2
        PA = lambda t: ps[:, t % 4, :]
        PE_ = lambda t: ps[:, 4 + t % 4, :]
        x_view = x.rearrange("(t p) d -> p t d", p=P)
        def gate(eng, sem, value, passed):
            eng.wait_ge(sem, value)
            eng.sem_inc(S[passed], 1)

        block = ctx.enter_context(nc.Block())

        @block.sync
        def _(sp):
            for c, (t0, t1) in enumerate(zip(XCUT, XCUT[1:])):
                sp.dma_start(xs[:, t0:t1, :], x_view[:, t0:t1, :]).then_inc(x_in[c], 16)
            for i in range(2 * T):
                half, jb = i // T, i % T
                if i >= RING:
                    old = i - RING
                    sp.wait_ge(S["lo_cast"] if old < T else S["hi_cast"], old % T + 1)
                sp.dma_start(strip[:, i % RING, :], adj[jb * P:(jb + 1) * P, half * (N // 2):(half + 1) * (N // 2)]
                             ).then_inc(strip_in[i % RING], 16)
                pair = (i - RING - 1) // 2
                if i % 2 == 1 and 0 <= pair < T // 2:
                    sp.dma_start(a8d[0:LOWP, :, 2 * pair:2 * pair + 2, :].rearrange("k p j i -> p k (j i)"),
                                 low[:, pair % LR].rearrange("p k j i -> p k (j i)")
                                 ).then_inc(low_out[pair % LR], 16)
            sp.wait_ge(S["hi_cast"], T)
            for k in range(LOWP):
                sp.dma_start(a8d[LOWP + k], res[:, k]).then_inc(S["res_out"], 16)
            for t in range(T):
                sp.wait_ge(S["x1_ready"], t + 1)
                sp.dma_start(x1d[t * P:(t + 1) * P, :], xs[:, t, :]).then_inc(S["x1_out"], 16)
                if t == T // 2:
                    sp.wait_ge(S["strip_used"], 2 * T)
                    sp.wait_ge(S["res_out"], 16 * LOWP)
                    for k in range(LR):
                        sp.wait_ge(low_out[k], 16 * T // 2 // LR)
                    for k in range(2):
                        sp.dma_start(pan[:, k], a8d[k]).then_inc(panel_in[k], 16)
            sp.wait_ge(S["slrow_ready"], 1)
            sp.dma_start(sld.rearrange("(t p) -> t p", p=P), slrow[:]).then_inc(S["sl_out"], 16)
            sp.wait_ge(S["x1_out"], 16 * T)
            for t in range(2):
                sp.dma_start(x1r[:, t, :], x1d[t * P:(t + 1) * P, :]).then_inc(x1r_in[t], 16)
            sp.wait_ge(S["sl_out"], 16)
            for s in range(2):
                sp.dma_start(slb[:, s, :], sld[s * PW:(s + 1) * PW].partition_broadcast(P)).then_inc(slb_in[s], 16)

            def sp_panel(s, slot):
                gate(sp, S["t_ready"], s * NCH + NCH, "passed_sp")
                gate(sp, S["a_done"], s * 2 + 2, "passed_sp")
                sp.dma_start(pan[:, slot], a8d[s + 2]).then_inc(panel_in[slot], 16)
                sp.dma_start(slb[:, slot, :], sld[bass.ds(s * PW + 2 * PW, PW)].partition_broadcast(P)
                             ).then_inc(slb_in[slot], 16)

            def sp_rows(s, last):
                for e in range(2):
                    gate(sp, S["out_ready"], s * 2 + e + 1, "passed_sp")
                    sp.dma_start(out[bass.ds(s * PW + e * P, P), :], ot[:, e, :]).then_inc(out_sent[e], 16)
                    if not last:
                        gate(sp, S["x1r_used"], s * 2 + e + 1, "passed_sp")
                        sp.dma_start(x1r[:, e, :], x1d[bass.ds(s * PW + PW + e * P, P), :]).then_inc(x1r_in[e], 16)

            with sp.Fori(0, NPAN // 2 - 1) as k:
                for m in range(2):
                    sp_panel(k * 2 + m, m)
                    sp_rows(k * 2 + m, False)
            sp_rows(NPAN - 2, False)
            sp_rows(NPAN - 1, True)
            for e in range(2):
                sp.wait_ge(out_sent[e], 16 * NPAN)

        @block.gpsimd
        def _(pool):
            pool.memset(ident[:], 0.0).then_inc(S["pool_step"], 1)
            pool.wait_ge(S["pool_step"], 1)
            pool.affine_select(out=ident[:], in_=ident[:], compare_op=ALU.not_equal, fill=1.0, base=0,
                               pattern=[[-1, P]], channel_multiplier=1).then_inc(S["const_ready"], 1)
            pool.wait_ge(S["const_ready"], 2)
            pool.wait_ge(S["xmax_part"], 1)
            pool.partition_all_reduce(sc[:, XALL], sc[:, XMX], P, RMAX).then_inc(S["xmax_all"], 1)
            pool.wait_ge(S["wsq_ready"], 1)
            pool.partition_all_reduce(wsum[:], wsq[:, 1, :], P, RADD).then_inc(S["wsum_ready"], 1)
            pool.wait_ge(S["wnorm_ready"], 1)
            pool.tensor_tensor(sc[:, WN], sc[:, WMX], sc[:, MH], ALU.pow).then_inc(S["alpha_pow"], 1)
            for t in range(T):
                pool.wait_ge(S["stat_ready"], t + 1)
                pool.tensor_tensor(lnst[:, t % 2, 9:10], lnst[:, t % 2, 8:9], sc[:, MH], ALU.pow
                                   ).then_inc(S["rstd_ready"], 1)
            pool.wait_ge(S["nsr_max"], 1)
            pool.partition_all_reduce(sc[:, NMAX], sc[:, NM], P, RMAX).then_inc(S["nmax_ready"], 1)

            def pool_rstd(t, e):
                gate(pool, S["ystat_ready"], t + 1, "passed_pool")
                pool.tensor_tensor(sc1[:, e, RS], sc1[:, e, VE], sc[:, MH], ALU.pow
                                   ).then_inc(S["yrstd_ready"], 1)

            with pool.Fori(0, T // 2) as k:
                for e in range(2):
                    pool_rstd(k * 2 + e, e)

        @block.scalar
        def _(act):
            def load_weights():
                kp = lambda a, c: a.rearrange("o (s k p) -> s p (o k)", s=2, p=P)[c]
                act.dma_start(wp[:, :, 0:D], Wg.rearrange("(k p) d -> p k d", p=P)).then_inc(S["wts_in"], 16)
                act.dma_start(wp[:, :, WG:WC], Wsa.rearrange("(k p) d -> p k d", p=P)).then_inc(S["wts_in"], 16)
                with nc.allow_non_contiguous_dma(reason="256 weights, one column each"):
                    for c, (a, s) in enumerate(((Wa, 0), (Wb, 0), (Wa, 1), (Wb, 1))):
                        act.dma_start(wp[:, :, D + c], kp(a, s)).then_inc(S["wts_in"], 16)
                act.dma_start(asab[:], asa.rearrange("o d -> (o d)").partition_broadcast(P)).then_inc(S["wts_in"], 16)
                act.dma_start(w0[:], W0.rearrange("(k p) d -> p k d", p=P)).then_inc(S["wts_in"], 16)
                act.dma_start(b0b[:], b0.partition_broadcast(P)).then_inc(S["wts_in"], 16)
                act.dma_start(bgb[:], bg.partition_broadcast(P)).then_inc(S["wts_in"], 16)
                act.dma_start(sc[:, BAB.start:BAB.start + 1], ba.partition_broadcast(P)).then_inc(S["wts_in"], 16)
                act.dma_start(sc[:, BAB.start + 1:BAB.stop], bb.partition_broadcast(P)).then_inc(S["wts_in"], 16)

            act.wait_ge(S["sx_ready"], 1)
            for jb in range(T):
                act.activation(y[:, jb, 0, :], xs[:, jb, :], ACT.Copy, scale=sc[:, SX]).then_inc(S["yhi_ready"], 1)

            def evac(half):
                act.wait_ge(S["strip_used"], T * (half + 1))
                for dh in range(KD):
                    for g in (NG2 * half, NG2 * half + 2):
                        act.copy(acct[g][:, dh, :], ps[:, sum_bank(g, dh), :]).then_inc(S["evac_act"], 1)

            def hi_cast(jb):
                i = T + jb
                act.wait_ge(strip_in[i % RING], 16 * (i // RING + 1))
                act.activation(res[:, :, jb, :], strip[:, i % RING, :].rearrange("p (k i) -> p k i", i=PW),
                               ACT.Copy, scale=float(EDGE - NONE), bias=float(NONE), accum_out=dega[:, jb:jb + 1]).then_inc(S["hi_cast"], 1)

            hi_cast(0)
            evac(0)
            for jb in range(1, T):
                hi_cast(jb)
                if jb == T // 2:
                    for c in range(LR):
                        act.wait_ge(low_out[c], 16 * T // 2 // LR)
                    load_weights()

            def z_scale(t):
                if t >= 2:
                    act.wait_ge(S["zt_done"], t - 1)
                act.activation(zx[:, t % 2, :], xs[:, t, :], ACT.Copy, scale=zs[:, t:t + 1]).then_inc(S["zx_ready"], 1)

            def x1t_copy(t):
                act.wait_ge(S["x1t_done"], t + 1)
                act.copy(x1t[:, t % 2].rearrange("p k i -> p (k i)"), ps[:, BT, 0:D]
                         ).then_inc(S["x1t_ready"], 1)

            def proj_copies(t):
                act.wait_ge(S["proj_done"], t + 1)
                act.copy(ex[:, t, :], ps[:, BG(t), GC:WG])
                act.activation(fa[:, t, 0, :], ps[:, BG(t), 0:GC], ACT.Copy, scale=sc[:, AL]
                               ).then_inc(S["ghi_ready"], 1)
                act.copy(h[:, t, :], ps[:, BH(t), 0:D]).then_inc(S["h_ready"], 1)

            act.wait_ge(S["scale_ready"], 1)
            for t in range(2):
                z_scale(t)
            evac(1)
            act.wait_ge(S["qa_ready"], 1)
            for n in range(T + 2):
                if n < T - 2:
                    z_scale(n + 2)
                if n >= 2:
                    proj_copies(n - 2)
                if 1 <= n <= T:
                    x1t_copy(n - 1)
            act.wait_ge(S["arg_ready"], 1)
            act.activation(q[:], tq[:], ACT.Exp, scale=SLOPE)
            act.activation(rr[:], tb[:], ACT.Exp, scale=-1.0).then_inc(S["pq_ready"], 1)
            act.wait_ge(S["qa_ready"], 2)
            for t in range(T):
                act.activation(fb[:, t, 0, 0:D], h[:, t, :], ACT.Copy, scale=qa[:, t:t + 1]
                               ).then_inc(S["fbhi_ready"], 1)

            def e_chunk(s, slot, c):
                gate(act, S["t_ready"], s * NCH + c + 1, "passed_act")
                act.activation(ec[:, c % ER], ec[:, c % ER], ACT.Exp, scale=-(1 - SLOPE), bias=sc[:, E8]
                               ).then_inc(S["e_ready"], 1)
                gate(act, S["e_ready"], s * NCH + c + 1, "passed_act")
                act.activation(em[:, slot, 0, c * CH:(c + 1) * CH, :], ec[:, c % ER], ACT.Copy, scale=MU
                               ).then_inc(S["ehi_ready"], 1)

            def gates(t, m):
                e = m % 2
                gate(act, S["a_done"], t + 1, "passed_act")
                for c in range(2):
                    act.activation(sc1[:, e, 12 + c:13 + c], PA(m)[:, D + c:D + c + 1], ACT.Tanh,
                                   scale=sc[:, HINVA], bias=rab[:, bass.ds(t, 1), c]).then_inc(S["th_ready"], 1)
                gate(act, S["th_ready"], t * 2 + 2, "passed_act")
                act.activation(sc1[:, e, ATT], sc1[:, e, TH], ACT.Copy, scale=0.5, bias=0.5
                               ).then_inc(S["att_ready"], 1)

            def gated(t, m):
                e = m % 2
                gate(act, S["att_ready"], t + 1, "passed_act")
                gate(act, S["w_ready"], t + 1, "passed_act")
                act.activation(wb[:, e, :], w[:, e, :], ACT.Copy, scale=sc1[:, e, 11:12]).then_inc(S["wb_ready"], 1)

            def sigmoid(t, m):
                e = m % 2
                gate(act, S["epi_read"], t + 1, "passed_act")
                act.activation(sg[:, e, :], w[:, e, :], ACT.Tanh, scale=0.5).then_inc(S["sg_ready"], 1)

            def act_panel(s, m):
                gates(s * 2, 2 * m)
                gate(act, S["bc_done"], s * 2, "passed_act")
                e_chunk(s + 1, 1 - m, 0)
                gated(s * 2, 2 * m)
                e_chunk(s + 1, 1 - m, 1)
                sigmoid(s * 2, 2 * m)
                gates(s * 2 + 1, 2 * m + 1)
                e_chunk(s + 1, 1 - m, 2)
                gated(s * 2 + 1, 2 * m + 1)
                e_chunk(s + 1, 1 - m, 3)
                sigmoid(s * 2 + 1, 2 * m + 1)

            act.wait_ge(S["x1_out"], 16 * T)
            for c in range(NCH):
                e_chunk(0, 0, c)
            for t in range(2):
                gates(t, t)
                gated(t, t)
            act.wait_ge(S["feat_ready"], T)
            for c in range(NCH):
                e_chunk(1, 1, c)
            for t in range(2):
                sigmoid(t, t)
            act_panel(1, 1)
            with act.Fori(1, NPAN // 2 - 1) as k:
                act_panel(k * 2, 0)
                act_panel(k * 2 + 1, 1)
            act_panel(NPAN - 2, 0)
            for t in range(N // P - 2, N // P):
                gates(t, t % 4)
                gated(t, t % 4)
            for t in range(N // P - 2, N // P):
                sigmoid(t, t % 4)

        @block.vector
        def _(dve):
            st = Steps(dve, S["dve_step"])
            dve.memset(sc[:, MH], -0.5)
            dve.memset(sc[:, CNONE], float(NONE))
            dve.memset(sc[:, E8], EDGE * (1 - SLOPE)).then_inc(S["const_ready"], 1)
            for c, (t0, t1) in enumerate(zip(XCUT, XCUT[1:])):
                dve.wait_ge(x_in[c], 16)
                st.then(dve.tensor_reduce(sc[:, c:c + 1], xs[:, t0:t1, :].rearrange("p t d -> p (t d)"),
                                          AX, ALU.max, apply_absolute_value=True))
            st.sync()
            dve.tensor_reduce(sc[:, XMX], sc[:, XM], AX, ALU.max).then_inc(S["xmax_part"], 1)
            dve.wait_ge(S["xmax_all"], 1)
            st.then(dve.tensor_scalar(sc[:, XG], sc[:, XALL], 1e-30, 1.0 / F16_TOP, ALU.max, ALU.mult))
            st.sync()
            st.then(dve.tensor_copy(sc[:, ISX], sc[:, XG]))
            dve.reciprocal(sc[:, SX], sc[:, XG]).then_inc(S["sx_ready"], 1)
            dve.wait_ge(S["sx_ready"], 1)

            def weight_columns():
                dve.wait_ge(S["wts_in"], 16 * 12)
                for k in range(KD):
                    for c in range(2):
                        st.then(dve.scalar_tensor_tensor(out=wsum[:, 0:D], in0=wp[:, k, WG:WC], scalar=1.0,
                                                         in1=asab[:, c * D:(c + 1) * D], op0=ALU.mult, op1=ALU.mult,
                                                         accum_out=wp[:, k, GC + 2 + c:GC + 3 + c]))
                        st.sync()
                flat = lambda a: a.rearrange("p k c -> p (k c)")
                st.then(dve.tensor_tensor(flat(wsq[:]), flat(wp[:]), flat(wp[:]), ALU.mult))
                st.sync()
                dve.tensor_tensor(wsq[:, 1, :], wsq[:, 0, :], wsq[:, 1, :], ALU.add).then_inc(S["wsq_ready"], 1)

            def weight_norm():
                dve.wait_ge(S["wsum_ready"], 1)
                st.then(dve.tensor_reduce(sc[:, TMP], wsum[:], AX, ALU.max))
                st.sync()
                dve.tensor_scalar(sc[:, WMX], sc[:, TMP], 1e-30, None, ALU.max).then_inc(S["wnorm_ready"], 1)

            def weight_scale():
                dve.wait_ge(S["alpha_pow"], 1)
                st.then(dve.tensor_scalar(sc[:, AL], sc[:, WN], F16_TOP / D ** 0.5, None, ALU.mult))
                st.sync()
                st.then(dve.reciprocal(sc[:, IAL], sc[:, AL]))
                st.sync()
                st.then(dve.tensor_scalar(sc[:, HINVA], sc[:, IAL], 0.5 / EDGE_VAL, None, ALU.mult))
                dve.tensor_scalar(sc[:, INVA], sc[:, IAL], 1.0 / EDGE_VAL, None, ALU.mult).then_inc(S["qa_ready"], 1)

            for jb in range(T):
                pair, jj = jb // 2, jb % 2
                dve.wait_ge(strip_in[jb % RING], 16 * (jb // RING + 1))
                if pair >= LR and jj == 0:
                    dve.wait_ge(low_out[pair % LR], 16 * (pair // LR))
                    dve.wait_ge(S["strip_used"], 2 * (pair - LR) + 2)
                dve.scalar_tensor_tensor(out=low[:, pair % LR, :, jj, :],
                                         in0=strip[:, jb % RING, :].rearrange("p (k i) -> p k i", i=PW),
                                         scalar=float(EDGE - NONE), op0=ALU.mult, op1=ALU.add,
                                         in1=sc[:, CNONE].unsqueeze(2).to_broadcast([P, LOWP, PW]),
                                         accum_out=degv[:, jb:jb + 1]).then_inc(S["lo_cast"], 1)
                dve.wait_ge(S["yhi_ready"], jb + 1)
                dve.scalar_tensor_tensor(out=y[:, jb, 1, :], in0=xs[:, jb, :], scalar=sc[:, SX],
                                         in1=y[:, jb, 0, :], op0=ALU.mult, op1=ALU.subtract
                                         ).then_inc(S["ylo_ready"], 1)

            def evac(g, dh):
                dve.tensor_copy(acct[g][:, dh, :], ps[:, sum_bank(g, dh), :]).then_inc(S["evac_dve"], 1)

            dve.wait_ge(S["strip_used"], T)
            for dh in range(KD):
                for g in (1, 3):
                    evac(g, dh)
            weight_columns()
            weight_norm()
            weight_scale()
            dve.wait_ge(S["hi_cast"], T)
            dve.wait_ge(S["lo_cast"], T)
            st.then(dve.tensor_tensor(deg[:], degv[:], dega[:], ALU.add))
            st.sync()
            st.then(dve.tensor_scalar(deg[:], deg[:], float(-N * NONE), 1.0 / (EDGE - NONE), ALU.add, ALU.mult))
            st.sync()
            st.then(dve.tensor_scalar(deg[:], deg[:], 1.0, None, ALU.max))
            st.sync()
            st.then(dve.tensor_scalar(zs[:], deg[:], 1.0, sc[:, SX], ALU.add, ALU.mult))
            st.then(dve.reciprocal(us[:], deg[:]))
            st.sync()
            st.then(dve.tensor_scalar(zs[:], zs[:], EDGE_VAL, None, ALU.mult))
            dve.tensor_scalar(us[:], us[:], sc[:, ISX], 1.0 / EDGE_VAL, ALU.mult, ALU.mult).then_inc(S["scale_ready"], 1)
            st.sync()
            dve.wait_ge(S["scale_ready"], 1)

            def add_share(t):
                g, tt = t // TG, t % TG
                a = acct[g][:, :, tt * P:(tt + 1) * P]
                dve.wait_ge(S["evac_act"], 8 if g >= NG2 else 4)
                dve.wait_ge(S["evac_dve"], 8 if g >= NG2 else 4)
                dve.wait_ge(S["zt_done"], t + 1)
                dve.tensor_tensor(a, a, ps[:, BZ, 0:D].rearrange("p (k i) -> p k i", k=KD), ALU.add
                                  ).then_inc(S["acct_ready"], 1)

            def g_lo(t):
                dve.wait_ge(S["ghi_ready"], t + 1)
                dve.scalar_tensor_tensor(out=fa[:, t, 1, :], in0=ps[:, BG(t), 0:GC], scalar=sc[:, AL],
                                         in1=fa[:, t, 0, :], op0=ALU.mult, op1=ALU.subtract
                                         ).then_inc(S["glo_ready"], 1)

            def normalize(t):
                dve.wait_ge(S["rstd_ready"], t + 1)
                ln = lnst[:, t % 2, :]
                dve.tensor_scalar(xs[:, t, :], xs[:, t, :], ln[:, 6:7], ln[:, RS], ALU.subtract, ALU.mult
                                  ).then_inc(S["x1_ready"], 1)

            dve.wait_ge(S["strip_used"], 2 * T)
            evac(5, 0)
            add_share(0)
            for g, dh in ((7, 0), (5, 1), (7, 1)):
                evac(g, dh)
            for n in range(T):
                e = n % 2
                u = ps[:, BU(n), 0:D]
                ln = lnst[:, e, :]
                dve.wait_ge(S["u_done"], n + 1)
                st.then(dve.scalar_tensor_tensor(out=u, in0=u, scalar=us[:, n:n + 1], in1=b0b[:], op0=ALU.mult,
                                                 op1=ALU.add))
                if n >= 1:
                    normalize(n - 1)
                if n >= 3:
                    g_lo(n - 3)
                st.sync()
                dve.scalar_tensor_tensor(out=xs[:, n, :], in0=u, scalar=0.0, in1=xs[:, n, :], op0=ALU.max,
                                         op1=ALU.add).then_inc(S["r2_done"], 1)
                if n < T - 1:
                    add_share(n + 1)
                dve.wait_ge(S["r2_done"], n + 1)
                st.then(dve.bn_stats(ln[:, BN], xs[:, n, :]))
                st.sync()
                st.then(dve.bn_aggr(ln[:, MV], ln[:, BN]))
                st.sync()
                dve.tensor_scalar(ln[:, VE], ln[:, 7:8], EPS, None, ALU.add).then_inc(S["stat_ready"], 1)
            normalize(T - 1)
            for t in range(T - 3, T):
                g_lo(t)

            dve.wait_ge(S["h_ready"], T)
            dve.wait_ge(S["u_done"], T)
            dve.wait_ge(S["res_out"], 16 * LOWP)
            dve.tensor_scalar(nsr[:], ex[:, :, 3], -1.0, None, ALU.mult).then_inc(S["nsr_ready"], 1)
            dve.wait_ge(S["nsr_ready"], 1)
            dve.tensor_reduce(sc[:, NM], nsr[:], AX, ALU.max).then_inc(S["nsr_max"], 1)
            dve.tensor_copy(slc[:], ex[:, :, 2]).then_inc(S["sl_ready"], 1)
            st.then(dve.tensor_scalar(sr8[:], ex[:, :, 3], float(EDGE), None, ALU.add))
            for c in range(2):
                st.then(dve.tensor_scalar(rab[:, :, c], ex[:, :, c], sc[:, BAB.start + c:BAB.start + c + 1], 0.5,
                                          ALU.add, ALU.mult))
            dve.wait_ge(S["nmax_ready"], 1)
            dve.wait_ge(S["slt_done"], 1)
            dve.tensor_scalar(slrow[:], ps[0:T, BU(0), 0:P], sc[0:T, NMAX], None, ALU.min
                              ).then_inc(S["slrow_ready"], 1)
            st.then(dve.tensor_scalar(tq[:], nsr[:], sc[:, NMAX], None, ALU.subtract))
            dve.wait_ge(S["sl_ready"], 1)
            st.then(dve.tensor_scalar(ta[:], slc[:], sc[:, NMAX], None, ALU.subtract))
            st.sync()
            dve.scalar_tensor_tensor(out=tb[:], in0=ta[:], scalar=SLOPE, in1=ta[:], op0=ALU.mult, op1=ALU.max
                                     ).then_inc(S["arg_ready"], 1)
            dve.wait_ge(S["pq_ready"], 1)
            dve.tensor_scalar(qa[:], q[:], sc[:, AL], None, ALU.mult).then_inc(S["qa_ready"], 1)
            st.then(dve.tensor_scalar(fb[:, :, 0, D], q[:], KAPPA, None, ALU.mult))
            st.then(dve.tensor_scalar(rden[:], rr[:], 1.0 / (MU * KAPPA), None, ALU.mult))
            st.then(dve.tensor_scalar(rnum[:], rr[:], sc[:, IAL], 1.0 / MU, ALU.mult, ALU.mult))
            dve.wait_ge(S["qa_ready"], 2)
            st.sync()
            st.then(dve.scalar_tensor_tensor(out=fb[:, :, 1, D], in0=q[:], scalar=KAPPA, in1=fb[:, :, 0, D],
                                             op0=ALU.mult, op1=ALU.subtract))
            for t in range(T):
                dve.wait_ge(S["fbhi_ready"], t + 1)
                dve.scalar_tensor_tensor(out=fb[:, t, 1, 0:D], in0=h[:, t, :], scalar=qa[:, t:t + 1],
                                         in1=fb[:, t, 0, 0:D], op0=ALU.mult, op1=ALU.subtract
                                         ).then_inc(S["feat_ready"], 1)

            def relu_chunk(s, slot, c):
                if s is not PEELED:
                    gate(dve, S["elo_ready"], s * NCH + c + 1 - ER, "passed_dve")
                for jj in range(CH):
                    jb = c * CH + jj
                    t_ = dve.scalar_tensor_tensor(out=ec[:, c % ER, jj, :], in0=slb[:, slot, :],
                                                  scalar=sr8[:, jb:jb + 1], in1=pan[:, slot, jb, :],
                                                  op0=ALU.add, op1=ALU.max)
                t_.then_inc(S["t_ready"], 1)

            def low_chunk(s, slot, c):
                gate(dve, S["ehi_ready"], s * NCH + c + 1, "passed_dve")
                rows = slice(c * CH, (c + 1) * CH)
                dve.scalar_tensor_tensor(out=em[:, slot, 1, rows, :], in0=ec[:, c % ER], scalar=MU,
                                         in1=em[:, slot, 0, rows, :], op0=ALU.mult, op1=ALU.subtract
                                         ).then_inc(S["elo_ready"], 1)

            def panel_waits(slot, nth):
                gate(dve, panel_in[slot], nth * 16, "passed_dve")
                gate(dve, slb_in[slot], nth * 16, "passed_dve")

            of_t = lambda v, t: v[:, bass.ds(t, 1)]

            def epi_w(t, m):
                gate(dve, S["att_ready"], t + 1, "passed_dve")
                dve.scalar_tensor_tensor(out=w[:, m % 2, :], in0=PA(m)[:, 0:D], scalar=sc[:, INVA], in1=bgb[:],
                                         op0=ALU.mult, op1=ALU.add).then_inc(S["w_ready"], 1)

            def epi_attend(t, m):
                s1 = sc1[:, m % 2, :]
                gate(dve, S["bc_done"], t + 1, "passed_dve")
                st.then(dve.tensor_scalar(s1[:, D2], PE_(m)[:, D:D + 1], of_t(rden, t), EPS, ALU.mult, ALU.add))
                st.sync()
                st.then(dve.reciprocal(s1[:, REC], s1[:, D2]))
                st.sync()
                st.then(dve.tensor_scalar(s1[:, CE], s1[:, REC], of_t(rnum, t), s1[:, 10:11], ALU.mult, ALU.mult))
                st.sync()
                gate(dve, S["wb_ready"], t + 1, "passed_dve")
                dve.scalar_tensor_tensor(out=w[:, m % 2, :], in0=PE_(m)[:, 0:D], scalar=s1[:, CE],
                                         in1=wb[:, m % 2, :], op0=ALU.mult, op1=ALU.add).then_inc(S["epi_read"], 1)

            def epi_sum(t, m, nth):
                e = m % 2
                s1 = sc1[:, e, :]
                gate(dve, S["sg_ready"], t + 1, "passed_dve")
                gate(dve, x1r_in[e], nth * 16, "passed_dve")
                dve.scalar_tensor_tensor(out=sg[:, e, :], in0=sg[:, e, :], scalar=0.5, in1=x1r[:, e, :],
                                         op0=ALU.mult, op1=ALU.add).then_inc(S["x1r_used"], 1)
                gate(dve, S["x1r_used"], t + 1, "passed_dve")
                st.then(dve.bn_stats(s1[:, BN], sg[:, e, :]))
                gate(dve, S["dve_step"], st.n + st.base, "passed_dve")
                st.then(dve.bn_aggr(s1[:, MV], s1[:, BN]))
                st.sync()
                dve.tensor_scalar(s1[:, VE], s1[:, 7:8], EPS, None, ALU.add).then_inc(S["ystat_ready"], 1)

            def epi_norm(t, m, nth, first=False):
                e = m % 2
                s1 = sc1[:, e, :]
                gate(dve, S["yrstd_ready"], t + 1, "passed_dve")
                if not first:
                    gate(dve, out_sent[e], nth * 16 - 16, "passed_dve")
                dve.tensor_scalar(ot[:, e, :], sg[:, e, :], s1[:, 6:7], s1[:, RS], ALU.subtract, ALU.mult
                                  ).then_inc(S["out_ready"], 1)

            PEELED = 0

            def panel_step(s, m, nth, first=False):
                n = 1 - m
                a, b = s * 2, s * 2 + 1
                panel_waits(n, nth)
                relu_chunk(s + 1, n, 0)
                epi_norm(a - 1, 2 * n + 1, s, first)
                epi_w(a, 2 * m)
                relu_chunk(s + 1, n, 1)
                low_chunk(s + 1, n, 0)
                relu_chunk(s + 1, n, 2)
                epi_attend(a, 2 * m)
                low_chunk(s + 1, n, 1)
                epi_sum(a, 2 * m, s + 1)
                epi_w(b, 2 * m + 1)
                relu_chunk(s + 1, n, 3)
                epi_norm(a, 2 * m, s + 1)
                low_chunk(s + 1, n, 2)
                epi_attend(b, 2 * m + 1)
                low_chunk(s + 1, n, 3)
                epi_sum(b, 2 * m + 1, s + 1)

            for s in range(2):
                panel_waits(s, 1)
                for c in range(NCH):
                    relu_chunk(PEELED if s == 0 else s, s, c)
                    if c >= 1:
                        low_chunk(s, s, c - 1)
                low_chunk(s, s, NCH - 1)
                if s == 0:
                    for t in range(2):
                        epi_w(t, t)
            for t in range(2):
                epi_attend(t, t)
                epi_sum(t, t, 1)
            epi_norm(0, 0, 1, first=True)
            panel_step(1, 1, 2, first=True)
            n0 = st.n
            with dve.Fori(1, NPAN // 2 - 1) as k:
                st.n, st.base = n0, k * PER_PAIR - PER_PAIR
                panel_step(k * 2, 0, k + 1)
                panel_step(k * 2 + 1, 1, k + 2)
                assert st.n - n0 == PER_PAIR, st.n - n0
            st.n, st.base = n0 + (NPAN // 2 - 2) * PER_PAIR, 0
            panel_step(NPAN - 2, 0, NPAN // 2)
            epi_norm(T - 3, 1, NPAN - 1)
            for t in range(T - 2, T):
                epi_w(t, t % 4)
            for t in range(T - 2, T):
                epi_attend(t, t % 4)
                epi_sum(t, t % 4, NPAN)
                epi_norm(t, t % 4, NPAN)

        @block.tensor
        def _(pe):
            pe.wait_ge(S["const_ready"], 2)
            for i in range(2 * T):
                half, jb = i // T, i % T
                pe.wait_ge(S["hi_cast" if half else "lo_cast"], jb + 1)
                if not half:
                    pe.wait_ge(S["ylo_ready"], jb + 1)
                for dh in range(KD):
                    for part in range(2):
                        for g in range(NG2):
                            if i == T and part == 0:
                                pe.wait_ge(S["evac_dve" if g % 2 else "evac_act"], 2 * dh + g // 2 + 1)
                            a = res[:, 2 * g:2 * g + 2, jb, :] if half else low[:, jb // 2 % LR, 2 * g:2 * g + 2, jb % 2, :]
                            mm = pe.matmul(ps[:, sum_bank(g, dh), :], y[:, jb, part, dh * P:(dh + 1) * P], a.bitcast(F8),
                                           start=(jb == 0 and part == 0), stop=(jb == T - 1 and part == 1))
                mm.then_inc(S["strip_used"], 1)

            def z_step(t):
                pe.wait_ge(S["zx_ready"], t + 1)
                if t >= 1:
                    pe.wait_ge(S["acct_ready"], t)
                else:
                    pe.wait_ge(S["evac_dve"], 5)
                for k in range(KD):
                    mm = pe.transpose(ps[:, BZ, k * P:(k + 1) * P], zx[:, t % 2, k * P:(k + 1) * P], ident[:])
                mm.then_inc(S["zt_done"], 1)

            def u_step(t):
                g, tt = t // TG, t % TG
                pe.wait_ge(S["acct_ready"], t + 1)
                if t < 2:
                    pe.wait_ge(S["evac_act"], 7)
                else:
                    pe.wait_ge(S["r2_done"], t - 1)
                for k in range(KD):
                    mm = pe.matmul(ps[:, BU(t), 0:D], acct[g][:, k, tt * P:(tt + 1) * P],
                                   w0[:, k, :], start=(k == 0), stop=(k == KD - 1))
                mm.then_inc(S["u_done"], 1)

            def t_step(t):
                pe.wait_ge(S["x1_ready"], t + 1)
                if t >= 1:
                    pe.wait_ge(S["x1t_ready"], t)
                else:
                    pe.wait_ge(S["evac_dve"], 7)
                for k in range(KD):
                    mm = pe.transpose(ps[:, BT, k * P:(k + 1) * P], xs[:, t, k * P:(k + 1) * P], ident[:])
                mm.then_inc(S["x1t_done"], 1)

            def p_step(t):
                pe.wait_ge(S["x1t_ready"], t + 1)
                if t < 2:
                    pe.wait_ge(S["evac_act"], 8)
                    pe.wait_ge(S["evac_dve"], 8)
                else:
                    pe.wait_ge(S["h_ready"], t - 1)
                    pe.wait_ge(S["glo_ready"], t - 1)
                for b, c0, c1 in ((BG(t), 0, WG), (BH(t), WG, WC)):
                    for k in range(KD):
                        mm = pe.matmul(ps[:, b, 0:c1 - c0], x1t[:, t % 2, k, :], wp[:, k, c0:c1],
                                       start=(k == 0), stop=(k == KD - 1))
                mm.then_inc(S["proj_done"], 1)

            z_step(0)
            for n in range(T + 2):
                if n < T:
                    u_step(n)
                if n < T - 1:
                    z_step(n + 1)
                if n >= 2:
                    p_step(n - 2)
                if 1 <= n <= T:
                    t_step(n - 1)

            pe.wait_ge(S["sl_ready"], 1)
            pe.transpose(ps[0:T, BU(0), 0:P], slc[:], ident[:]).then_inc(S["slt_done"], 1)

            def a_tile(m, slot):
                for jb in range(T):
                    for part in range(2):
                        mm = pe.matmul(PA(m)[:, 0:GC], pan[:, slot, jb, (m % 2) * P:(m % 2 + 1) * P].bitcast(F8),
                                       fa[:, jb, part, :], start=(jb == 0 and part == 0),
                                       stop=(jb == T - 1 and part == 1))
                mm.then_inc(S["a_done"], 1)

            def e_rows(m, slot, j0, j1):
                for jb in range(j0, j1):
                    for pe_part, f_part in ((0, 0), (0, 1), (1, 0)):
                        mm = pe.matmul(PE_(m)[:, 0:HC], em[:, slot, pe_part, jb, (m % 2) * P:(m % 2 + 1) * P],
                                       fb[:, jb, f_part, :], start=(jb == 0 and pe_part + f_part == 0),
                                       stop=(jb == T - 1 and pe_part == 1))
                return mm

            pe.wait_ge(S["glo_ready"], T)
            pe.wait_ge(S["slrow_ready"], 1)
            pe.wait_ge(S["h_ready"], T)
            for t in range(3):
                if t % 2 == 0:
                    pe.wait_ge(panel_in[t // 2], 16)
                a_tile(t, t // 2)

            def a_tiles(s, m, nth, first=False):
                if not first:
                    gate(pe, S["w_ready"], s * 2, "passed_pe")
                a_tile(2 * m + 3, 1 - m)
                gate(pe, panel_in[m], nth * 16, "passed_pe")
                gate(pe, S["w_ready"], s * 2 + 1, "passed_pe")
                a_tile(2 * m, m)

            def e_tiles(s, m, first=False):
                gate(pe, S["elo_ready"], s * NCH + NCH, "passed_pe")
                for e in range(2):
                    if not first:
                        gate(pe, S["epi_read"], s * 2 + e - 3, "passed_pe")
                    e_rows(2 * m + e, m, 0, T).then_inc(S["bc_done"], 1)

            pe.wait_ge(S["feat_ready"], T)
            for c in range(NCH):
                pe.wait_ge(S["elo_ready"], c + 1)
                for e in range(2):
                    mm = e_rows(e, 0, c * CH, (c + 1) * CH)
                    if c == NCH - 1:
                        mm.then_inc(S["bc_done"], 1)
            a_tiles(0, 0, 2, first=True)
            e_tiles(1, 1, first=True)
            a_tiles(1, 1, 2)
            with pe.Fori(1, NPAN // 2 - 1) as k:
                for m in range(2):
                    e_tiles(k * 2 + m, m)
                    a_tiles(k * 2 + m, m, k + 2)
            e_tiles(NPAN - 2, 0)
            pe.wait_ge(S["w_ready"], T - 4)
            a_tile(3, 1)
            e_tiles(NPAN - 1, 1)


PER_PAIR = 4 * 5


_INS = ['x', 'adj', 'L0_gnn_W', 'L0_gnn_b', 'L1_gnn_W_sa', 'L1_gnn_a_sa', 'L1_gnn_W_gcnb', 'L1_gnn_b_gcnb',
        'L1_gnn_Wa', 'L1_gnn_ba', 'L1_gnn_Wb', 'L1_gnn_bb']


def kernel(**inputs):
    import numpy as _np
    import concourse.bacc as _bacc
    from concourse import mybir as _mybir
    from concourse.bass_utils import run_bass_kernel_spmd as _run

    nc = _bacc.Bacc("TRN2", target_bir_lowering=False, num_devices=1)
    arrays, args = {}, []
    for name in _INS:
        a = _np.ascontiguousarray(inputs[name])
        arrays[f"in_{name}_dram"] = a
        args.append(nc.dram_tensor(f"in_{name}_dram", a.shape, _mybir.dt.from_np(a.dtype), kind="ExternalInput").ap())
    o = nc.dram_tensor("out_0_dram", (N, D), _mybir.dt.float32, kind="ExternalOutput").ap()
    build(nc, *args, o)
    r = _run(nc, [arrays], core_ids=[0])
    return r.results[0]["out_0_dram"]
```

```python
from contextlib import ExitStack

import numpy as np
import concourse.bass as bass
from concourse import mybir

ALU = mybir.AluOpType
ACT = mybir.ActivationFunctionType
AX = mybir.AxisListType.X
F32, F16, F8 = mybir.dt.float32, mybir.dt.float16, mybir.dt.float8e4
U8, U32 = mybir.dt.uint8, mybir.dt.uint32
RMAX = bass.bass_isa.ReduceOp.max
RADD = bass.bass_isa.ReduceOp.add

P = 128
N = 4096
D = 256
T = N // P
KD = D // P
PW = 256
NPAN = N // PW
LOWP = NPAN // 2
GW = 512
TG = GW // P
NG = N // GW
NG2 = NG // 2
RING = 4
LAST = 3
WTS = 12
WTS_AT = 18
CUTS = (4, 8, 20)
WARM = 30
CH = 8
NCH = T // CH
GC = D + 2
HC = D + 1
NEX = 4
WG = GC + NEX
WC = WG + D
EPS = 1e-5
F16_TOP = 32768.0
KAPPA = 16384.0
MU = 16384.0
X1S = 1024.0
PROJ = X1S * D ** 0.5
SLOPE = 0.01
EDGE, NONE = 8, 128
EDGE_VAL = 2.0 ** -6
XCUT = (0, 8, 16, 24, 28, 30, 32)
QS = 4
LAG = 12
ER = 4

PER_PAIR = 4 * 5

BASE = 16512
O_FA = 0
O_Y = O_FA + T * 2 * GC * 2
O_X = O_Y + T * 2 * D * 2
O_FB = O_X + T * D * 4
O_RES = O_FB + T * 2 * HC * 2
O_PERS = O_RES + T * N // 2
TOP = 229344 - BASE


class Steps:

    def __init__(self, eng, sem):
        self.eng, self.sem, self.n, self.base = eng, sem, 0, 0

    def then(self, ins):
        ins.then_inc(self.sem, 1)
        self.n += 1

    def sync(self):
        self.eng.wait_ge(self.sem, self.n + self.base)


def build(nc, x, adj, W0, b0, Wsa, asa, Wg, bg, Wa, ba, Wb, bb, out):
    def at(name, shape, dt, off):
        size = int(np.prod(shape[1:])) * mybir.dt.size(dt)
        assert off + size <= TOP, (name, off + size, TOP)
        return nc.alloc_sbuf_tensor_at(name, shape, dt, offset=BASE + off)

    class Area:

        def __init__(self, off, end):
            self.off, self.end = off, end

        def __call__(self, name, shape, dt):
            t = at(name, shape, dt, self.off)
            self.off += -(-int(np.prod(shape[1:])) * mybir.dt.size(dt) // 32) * 32
            assert self.off <= self.end, (name, self.off, self.end)
            return t

    fa = at("fa", [P, T, 2, GC], F16, O_FA)
    fb = at("fb", [P, T, 2, HC], F16, O_FB)
    y = at("y", [P, T, 2, D], F16, O_Y)
    xs = at("xs", [P, T, D], F32, O_X)
    strip = at("strip", [P, RING, N // 2], F32, O_FB)
    em = [at(f"em{m}", [P, 2, T, PW], F16, (O_X, O_Y)[m]) for m in range(2)]
    res = at("res", [P, LOWP, T, PW], U8, O_RES)
    area = Area(O_FA, O_FA + 16384)
    wsq = area("wsq", [P, KD, WC], F32)
    asab = area("asab", [P, 2 * D], F32)
    wsum = area("wsum", [P, WC], F32)
    wp = area("wp", [P, KD, WC], F32)
    O_ACCT = O_FA + 16384
    acct = [at(f"acct{g}", [P, KD, GW], F32, O_ACCT + g * KD * GW * 4) for g in range(NG2)]
    area = Area(O_Y, O_X)
    acct += [area(f"acct{g}", [P, KD, GW], F32) for g in range(NG2, NG)]
    x1t = area("x1t", [P, 2, 2, D], F16)
    lnst = area("lnst", [P, 2, 12], F32)
    pan = at("pan", [P, 2, T, PW], U8, O_RES)
    ec = at("ec", [P, ER, CH, PW], F32, O_RES + 4 * T * PW)
    area = Area(O_RES + 2 * T * PW, O_RES + 4 * T * PW)
    slb = area("slb", [P, 2, PW], F32)
    x1r = area("x1r", [P, 2, D], F32)
    w = area("w", [P, 2, D], F32)
    wb = area("wb", [P, 2, D], F32)
    sg = area("sg", [P, 2, D], F32)
    ot = area("ot", [P, 2, D], F32)
    nsr = area("nsr", [P, T], F32)
    slc = area("slc", [P, T], F32)
    sr8 = area("sr8", [P, T], F32)
    ta = area("ta", [P, T], F32)
    tb = area("tb", [P, T], F32)
    rr = area("rr", [P, T], F32)
    rden = area("rden", [P, T], F32)
    rnum = area("rnum", [P, T], F32)
    rab = area("rab", [P, T, 2], F32)
    slrow = area("slrow", [T, P], F32)
    sc1 = area("sc1", [P, 2, 32], F32)
    area = Area(O_PERS, TOP)
    wps = area("wps", [P, KD, 2, WC], F16)
    w0 = area("w0", [P, KD, D], F32)
    b0b = area("b0b", [P, D], F32)
    bgb = area("bgb", [P, D], F32)
    ident = area("ident", [P, P], F32)
    zx = area("zx", [P, 2, D], F32)
    ex = area("ex", [P, T, NEX], F32)
    q = area("q", [P, T], F32)
    qa = area("qa", [P, T], F32)
    degv = area("degv", [P, T], F32)
    dega = area("dega", [P, T], F32)
    deg = area("deg", [P, T], F32)
    zs = area("zs", [P, T], F32)
    us = area("us", [P, T], F32)
    sc = area("sc", [P, 32], F32)
    col = iter(range(32))
    column = lambda n=1: (lambda a: slice(a[0], a[-1] + 1))([next(col) for _ in range(n)])
    XM, BAB = column(len(XCUT) - 1), column(2)
    XMX, XALL, XG, SX, ISX = (column() for _ in range(5))
    TMP, WMX, WN, AL, IAL, WS = (column() for _ in range(6))
    INVA, HINVA, EXS, QSC, QB = (column() for _ in range(5))
    NM, NMAX, DFIRST = (column() for _ in range(3))
    MH, E8, CNONE = (column() for _ in range(3))
    BN, MV, VE, RS, ATT, TH, D2, REC, CE = (
        slice(0, 6), slice(6, 8), slice(8, 9), slice(9, 10), slice(10, 12), slice(12, 14), slice(14, 15),
        slice(15, 16), slice(16, 17))

    a8d = nc.dram_tensor("a8_scratch", [NPAN, P, T, PW], U8)
    x1d = nc.dram_tensor("x1_scratch", [N, D], F32)
    sld = nc.dram_tensor("sl_scratch", [N], F32)
    sl0d = nc.dram_tensor("sl0_scratch", [2 * PW], F32)

    with ExitStack() as ctx:
        ps = ctx.enter_context(nc.psum_tensor("ps", [P, 8, 512], F32))
        block_sem = lambda name: ctx.enter_context(nc.semaphore(name))
        S = {}
        for name in (
            "wts_in", "first_in", "first_cast", "wsq_ready", "wsum_ready", "wnorm_ready", "alpha_pow",
            "const_ready", "xmax_part", "xmax_all", "sx_ready", "lo_cast", "hi_cast", "scale_ready",
            "yhi_ready", "ylo_ready", "strip_used", "bank_done", "res_out", "share_ready", "share_t_done",
            "sums_ready", "evac_act", "evac_dve", "u_done", "r_ready", "stat_ready", "rstd_ready",
            "shift_ready", "x1_ready", "x1t_done", "x1t_ready", "x1t_lo_ready", "wps_ready", "proj_done",
            "ghi_ready", "q_ready", "qa_ready", "hhi_ready", "hlo_ready", "glo_ready", "x1_out", "nsr_ready",
            "nsr_max", "nmax_ready", "arg_ready", "rr_ready", "sl_ready", "slt_done", "slrow_ready", "sl_out",
            "sl0_out", "ex_ready", "alpha_ready", "relu_ready", "exp_done", "ehigh_ready", "elow_ready",
            "asum_done", "esum_done", "gates_ready", "tanh_ready", "w_ready", "gated_ready", "attend_done",
            "sigmoid_ready", "ystat_ready", "yrstd_ready", "out_ready", "dve_step", "pool_step", "passed_pe",
            "passed_dve", "passed_act", "passed_sp", "passed_pool", "x1r_used",
        ):
            S[name] = block_sem(name)
        several = lambda name, n: [block_sem(f"{name}{c}") for c in range(n)]
        x_in, strip_in, low_out = several("x_in", len(XCUT) - 1), several("strip_in", RING), several("low_out", T // QS)
        panel_in, slb_in, x1r_in, out_sent = (several(name, 2) for name in ("panel_in", "slb_in", "x1r_in", "out_sent"))

        sum_bank = lambda g, dh: 2 * (g % NG2) + dh
        BU, BZ, BT, BG, BH = lambda t: t % 2, 2, 3, lambda t: 4 + t % 2, lambda t: 6 + t % 2
        PA = lambda t: ps[:, t % 4, :]
        PH = lambda t: ps[:, 4 + t % 4, :]
        LAST_BANKS = ((5, 0), (4, 0), (5, 1), (4, 1), (6, 0), (7, 0), (6, 1), (7, 1))
        nth_bank = lambda g, dh: LAST_BANKS.index((g, dh)) + 1

        def evac_count(g, dh):
            return 4 + [b for b in LAST_BANKS if b[0] % 2 == g % 2].index((g, dh)) + 1
        x_view = x.rearrange("(t p) d -> p t d", p=P)

        def gate(eng, sem, value, passed):
            eng.wait_ge(sem, value)
            eng.sem_inc(S[passed], 1)

        block = ctx.enter_context(nc.Block())

        @block.sync
        def _(sp):
            def load_weights():
                kp = lambda a, c: a.rearrange("o (s k p) -> s p (o k)", s=2, p=P)[c]
                sp.dma_start(wp[:, :, 0:D], Wg.rearrange("(k p) d -> p k d", p=P)).then_inc(S["wts_in"], 16)
                sp.dma_start(wp[:, :, WG:WC], Wsa.rearrange("(k p) d -> p k d", p=P)).then_inc(S["wts_in"], 16)
                with nc.allow_non_contiguous_dma(reason="256 weights, one column each"):
                    for c, (a, s) in enumerate(((Wa, 0), (Wb, 0), (Wa, 1), (Wb, 1))):
                        sp.dma_start(wp[:, :, D + c], kp(a, s)).then_inc(S["wts_in"], 16)
                sp.dma_start(asab[:], asa.rearrange("o d -> (o d)").partition_broadcast(P)).then_inc(S["wts_in"], 16)
                sp.dma_start(w0[:], W0.rearrange("(k p) d -> p k d", p=P)).then_inc(S["wts_in"], 16)
                sp.dma_start(b0b[:], b0.partition_broadcast(P)).then_inc(S["wts_in"], 16)
                sp.dma_start(bgb[:], bg.partition_broadcast(P)).then_inc(S["wts_in"], 16)
                sp.dma_start(sc[:, BAB.start:BAB.start + 1], ba.partition_broadcast(P)).then_inc(S["wts_in"], 16)
                sp.dma_start(sc[:, BAB.start + 1:BAB.stop], bb.partition_broadcast(P)).then_inc(S["wts_in"], 16)

            for c, (t0, t1) in enumerate(zip(XCUT, XCUT[1:])):
                sp.dma_start(xs[:, t0:t1, :], x_view[:, t0:t1, :]).then_inc(x_in[c], 16)
            for c in range(2):
                sp.dma_start(strip[:, 0, c * N // 4:(c + 1) * N // 4], adj[0:P, c * N // 4:(c + 1) * N // 4]
                             ).then_inc(strip_in[0] if c else S["first_in"], 16)
            for i in range(2 * T):
                half, jb = i // T, i % T
                if i >= RING:
                    old = i - RING
                    sp.wait_ge(S["lo_cast"] if old < T else S["hi_cast"], old % T + 1)
                    if old == 0:
                        sp.wait_ge(S["first_cast"], 1)
                if i > 0:
                    sp.dma_start(strip[:, i % RING, :], adj[jb * P:(jb + 1) * P, half * (N // 2):(half + 1) * (N // 2)]
                                 ).then_inc(strip_in[i % RING], 16)
                if i == T + WTS_AT:
                    load_weights()
                b = (i - LAG) // QS
                if i % QS == LAG % QS and 0 <= b < T // QS:
                    sp.wait_ge(S["lo_cast"], QS * b + QS)
                    sp.dma_start(a8d[0:LOWP, :, QS * b:QS * b + QS, :].rearrange("k p j i -> p k (j i)"),
                                 res[:, :, QS * b:QS * b + QS, :].rearrange("p k j i -> p k (j i)")
                                 ).then_inc(low_out[b], 16)
            sp.wait_ge(S["hi_cast"], T)
            for k in range(LOWP):
                sp.dma_start(a8d[LOWP + k], res[:, k]).then_inc(S["res_out"], 16)
            for t in range(T):
                sp.wait_ge(S["x1_ready"], t + 1)
                sp.dma_start(x1d[t * P:(t + 1) * P, :], xs[:, t, :]).then_inc(S["x1_out"], 16)
                if t == T // 2:
                    sp.wait_ge(S["bank_done"], 2 * NG2)
                    sp.wait_ge(S["res_out"], 16 * LOWP)
                    for b in range(T // QS):
                        sp.wait_ge(low_out[b], 16)
                    for k in range(2):
                        sp.dma_start(pan[:, k], a8d[k]).then_inc(panel_in[k], 16)
                    sp.wait_ge(S["ex_ready"], 4)
                    with nc.allow_non_contiguous_dma(reason="512 values, once"):
                        sp.dma_start(sl0d.rearrange("(t p) -> p t", p=P), ex[:, 0:4, 2]).then_inc(S["sl0_out"], 16)
                    sp.wait_ge(S["sl0_out"], 16)
                    for k in range(2):
                        sp.dma_start(slb[:, k, :], sl0d[k * PW:(k + 1) * PW].partition_broadcast(P)
                                     ).then_inc(slb_in[k], 16)
            sp.wait_ge(S["slrow_ready"], 1)
            sp.dma_start(sld.rearrange("(t p) -> t p", p=P), slrow[:]).then_inc(S["sl_out"], 16)
            sp.wait_ge(S["x1_out"], 16 * T)
            for t in range(2):
                sp.dma_start(x1r[:, t, :], x1d[t * P:(t + 1) * P, :]).then_inc(x1r_in[t], 16)
            sp.wait_ge(S["sl_out"], 16)

            def sp_panel(s, slot):
                gate(sp, S["relu_ready"], s * NCH + NCH, "passed_sp")
                gate(sp, S["asum_done"], s * 2 + 2, "passed_sp")
                sp.dma_start(pan[:, slot], a8d[s + 2]).then_inc(panel_in[slot], 16)
                sp.dma_start(slb[:, slot, :], sld[bass.ds(s * PW + 2 * PW, PW)].partition_broadcast(P)
                             ).then_inc(slb_in[slot], 16)

            def sp_rows(s, last):
                for e in range(2):
                    gate(sp, S["out_ready"], s * 2 + e + 1, "passed_sp")
                    sp.dma_start(out[bass.ds(s * PW + e * P, P), :], ot[:, e, :]).then_inc(out_sent[e], 16)
                    if not last:
                        gate(sp, S["x1r_used"], s * 2 + e + 1, "passed_sp")
                        sp.dma_start(x1r[:, e, :], x1d[bass.ds(s * PW + PW + e * P, P), :]).then_inc(x1r_in[e], 16)

            with sp.Fori(0, NPAN // 2 - 1) as k:
                for m in range(2):
                    sp_panel(k * 2 + m, m)
                    sp_rows(k * 2 + m, False)
            sp_rows(NPAN - 2, False)
            sp_rows(NPAN - 1, True)
            for e in range(2):
                sp.wait_ge(out_sent[e], 16 * NPAN)

        @block.gpsimd
        def _(pool):
            pool.memset(ident[:], 0.0).then_inc(S["pool_step"], 1)
            pool.wait_ge(S["pool_step"], 1)
            pool.affine_select(out=ident[:], in_=ident[:], compare_op=ALU.not_equal, fill=1.0, base=0,
                               pattern=[[-1, P]], channel_multiplier=1).then_inc(S["const_ready"], 1)
            pool.wait_ge(S["const_ready"], 2)
            pool.wait_ge(S["xmax_part"], 1)
            pool.partition_all_reduce(sc[:, XALL], sc[:, XMX], P, RMAX).then_inc(S["xmax_all"], 1)
            pool.wait_ge(S["wsq_ready"], 1)
            pool.partition_all_reduce(wsum[:], wsq[:, 1, :], P, RADD).then_inc(S["wsum_ready"], 1)
            pool.wait_ge(S["wnorm_ready"], 1)
            pool.tensor_tensor(sc[:, WN], sc[:, WMX], sc[:, MH], ALU.pow).then_inc(S["alpha_pow"], 1)
            for t in range(T):
                pool.wait_ge(S["stat_ready"], t + 1)
                pool.tensor_tensor(lnst[:, t % 2, 9:10], lnst[:, t % 2, 8:9], sc[:, MH], ALU.pow
                                   ).then_inc(S["rstd_ready"], 1)
                pool.wait_ge(S["rstd_ready"], t + 1)
                pool.tensor_scalar(lnst[:, t % 2, 10:11], lnst[:, t % 2, 9:10], lnst[:, t % 2, 6:7], -1.0,
                                   ALU.mult, ALU.mult).then_inc(S["shift_ready"], 1)
            pool.wait_ge(S["nsr_max"], 1)
            pool.partition_all_reduce(sc[:, NMAX], sc[:, NM], P, RMAX).then_inc(S["nmax_ready"], 1)

            def pool_rstd(t, e):
                gate(pool, S["ystat_ready"], t + 1, "passed_pool")
                pool.tensor_tensor(sc1[:, e, RS], sc1[:, e, VE], sc[:, MH], ALU.pow
                                   ).then_inc(S["yrstd_ready"], 1)

            with pool.Fori(0, T // 2) as k:
                for e in range(2):
                    pool_rstd(k * 2 + e, e)

        @block.scalar
        def _(act):
            act.wait_ge(S["sx_ready"], 1)
            for jb in range(T):
                act.activation(y[:, jb, 0, :], xs[:, jb, :], ACT.Copy, scale=sc[:, SX]).then_inc(S["yhi_ready"], 1)
                if jb == 0:
                    act.wait_ge(strip_in[0], 16)
                    act.activation(res[:, LOWP // 2:LOWP, 0, :],
                                   strip[:, 0, N // 4:N // 2].rearrange("p (k i) -> p k i", i=PW), ACT.Copy,
                                   scale=float(EDGE - NONE), bias=float(NONE), accum_out=sc[:, DFIRST]
                                   ).then_inc(S["first_cast"], 1)

            def evac(g, dh):
                act.copy(acct[g][:, dh, :], ps[:, sum_bank(g, dh), :]).then_inc(S["evac_act"], 1)

            def evac_last(g, dh):
                act.wait_ge(S["bank_done"], nth_bank(g, dh))
                evac(g, dh)

            def hi_cast(jb):
                i = T + jb
                act.wait_ge(strip_in[i % RING], 16 * (i // RING + 1))
                act.wait_ge(S["strip_used"], jb + 1)
                act.wait_ge(low_out[jb // QS], 16)
                act.activation(res[:, :, jb, :], strip[:, i % RING, :].rearrange("p (k i) -> p k i", i=PW),
                               ACT.Copy, scale=float(EDGE - NONE), bias=float(NONE), accum_out=dega[:, jb:jb + 1]
                               ).then_inc(S["hi_cast"], 1)

            hi_cast(0)
            act.wait_ge(S["strip_used"], T)
            for dh in range(KD):
                for g in (0, 2):
                    evac(g, dh)
            for jb in range(1, T):
                hi_cast(jb)

            def z_scale(t):
                if t >= 2:
                    act.wait_ge(S["share_t_done"], t - 1)
                act.activation(zx[:, t % 2, :], xs[:, t, :], ACT.Copy, scale=zs[:, t:t + 1]
                               ).then_inc(S["share_ready"], 1)

            def normalize(t):
                act.wait_ge(S["shift_ready"], t + 1)
                act.activation(xs[:, t, :], xs[:, t, :], ACT.Identity, scale=lnst[:, t % 2, RS],
                               bias=lnst[:, t % 2, 10:11]).then_inc(S["x1_ready"], 1)

            def x1t_copy(t):
                act.wait_ge(S["x1t_done"], t + 1)
                if t >= 2:
                    act.wait_ge(S["proj_done"], t - 1)
                act.activation(x1t[:, t % 2, 0, :], ps[:, BT, 0:D], ACT.Copy, scale=X1S
                               ).then_inc(S["x1t_ready"], 1)

            def proj_copies(t):
                act.wait_ge(S["proj_done"], t + 1)
                act.activation(q[:, t:t + 1], ps[:, BG(t), GC + 3:WG], ACT.Exp, scale=sc[:, QSC], bias=sc[:, QB]
                               ).then_inc(S["q_ready"], 1)
                act.activation(ex[:, t, :], ps[:, BG(t), GC:WG], ACT.Copy, scale=sc[:, EXS]).then_inc(S["ex_ready"], 1)
                act.activation(fa[:, t, 0, :], ps[:, BG(t), 0:GC], ACT.Copy, scale=1.0 / PROJ
                               ).then_inc(S["ghi_ready"], 1)
                act.wait_ge(S["q_ready"], t + 1)
                act.activation(qa[:, t:t + 1], q[:, t:t + 1], ACT.Copy, scale=1.0 / PROJ).then_inc(S["qa_ready"], 1)
                act.wait_ge(S["qa_ready"], t + 1)
                act.activation(fb[:, t, 0, 0:D], ps[:, BH(t), 0:D], ACT.Copy, scale=qa[:, t:t + 1]
                               ).then_inc(S["hhi_ready"], 1)

            act.wait_ge(S["scale_ready"], 1)
            for t in range(2):
                z_scale(t)
            act.wait_ge(S["alpha_ready"], 1)
            for n in range(T + 2):
                if n == 0:
                    evac_last(4, 0)
                elif n == 1:
                    evac_last(4, 1)
                    evac_last(6, 0)
                if 1 <= n <= T:
                    normalize(n - 1)
                if n < T - 2:
                    z_scale(n + 2)
                if 1 <= n <= T:
                    x1t_copy(n - 1)
                if n == 1:
                    evac_last(6, 1)
                if n >= 2:
                    proj_copies(n - 2)

            def e_chunk(s, slot, c):
                gate(act, S["relu_ready"], s * NCH + c + 1, "passed_act")
                act.activation(ec[:, c % ER], ec[:, c % ER], ACT.Exp, scale=-(1 - SLOPE), bias=sc[:, E8]
                               ).then_inc(S["exp_done"], 1)
                gate(act, S["exp_done"], s * NCH + c + 1, "passed_act")
                act.activation(em[slot][:, 0, c * CH:(c + 1) * CH, :], ec[:, c % ER], ACT.Copy, scale=MU
                               ).then_inc(S["ehigh_ready"], 1)

            def gates(t, m):
                e = m % 2
                gate(act, S["asum_done"], t + 1, "passed_act")
                for c in range(2):
                    act.activation(sc1[:, e, 12 + c:13 + c], PA(m)[:, D + c:D + c + 1], ACT.Tanh,
                                   scale=sc[:, HINVA], bias=rab[:, bass.ds(t, 1), c]).then_inc(S["tanh_ready"], 1)
                gate(act, S["tanh_ready"], t * 2 + 2, "passed_act")
                act.activation(sc1[:, e, ATT], sc1[:, e, TH], ACT.Copy, scale=0.5, bias=0.5
                               ).then_inc(S["gates_ready"], 1)

            def gated(t, m):
                e = m % 2
                gate(act, S["gates_ready"], t + 1, "passed_act")
                gate(act, S["w_ready"], t + 1, "passed_act")
                act.activation(wb[:, e, :], w[:, e, :], ACT.Copy, scale=sc1[:, e, 11:12]).then_inc(S["gated_ready"], 1)

            def sigmoid(t, m):
                e = m % 2
                gate(act, S["attend_done"], t + 1, "passed_act")
                act.activation(sg[:, e, :], w[:, e, :], ACT.Tanh, scale=0.5).then_inc(S["sigmoid_ready"], 1)

            def act_panel(s, m):
                gates(s * 2, 2 * m)
                gate(act, S["esum_done"], s * 2, "passed_act")
                e_chunk(s + 1, 1 - m, 0)
                gated(s * 2, 2 * m)
                e_chunk(s + 1, 1 - m, 1)
                sigmoid(s * 2, 2 * m)
                gates(s * 2 + 1, 2 * m + 1)
                e_chunk(s + 1, 1 - m, 2)
                gated(s * 2 + 1, 2 * m + 1)
                e_chunk(s + 1, 1 - m, 3)
                sigmoid(s * 2 + 1, 2 * m + 1)

            act.wait_ge(S["x1_out"], 16 * T)
            for c in range(NCH):
                e_chunk(0, 0, c)
                if c == 0:
                    act.wait_ge(S["arg_ready"], 1)
                    act.activation(rr[:], tb[:], ACT.Exp, scale=-1.0).then_inc(S["rr_ready"], 1)
            for t in range(2):
                gates(t, t)
                gated(t, t)
            for c in range(NCH):
                e_chunk(1, 1, c)
            for t in range(2):
                sigmoid(t, t)
            act_panel(1, 1)
            with act.Fori(1, NPAN // 2 - 1) as k:
                act_panel(k * 2, 0)
                act_panel(k * 2 + 1, 1)
            act_panel(NPAN - 2, 0)
            for t in range(T - 2, T):
                gates(t, t % 4)
                gated(t, t % 4)
            for t in range(T - 2, T):
                sigmoid(t, t % 4)

        @block.vector
        def _(dve):
            st = Steps(dve, S["dve_step"])
            dve.memset(sc[:, MH], -0.5)
            dve.memset(sc[:, CNONE], float(NONE))
            dve.memset(sc[:, E8], EDGE * (1 - SLOPE)).then_inc(S["const_ready"], 1)
            for c, (t0, t1) in enumerate(zip(XCUT, XCUT[1:])):
                dve.wait_ge(x_in[c], 16)
                st.then(dve.tensor_reduce(sc[:, c:c + 1], xs[:, t0:t1, :].rearrange("p t d -> p (t d)"),
                                          AX, ALU.max, apply_absolute_value=True))
            st.sync()
            dve.tensor_reduce(sc[:, XMX], sc[:, XM], AX, ALU.max).then_inc(S["xmax_part"], 1)
            dve.wait_ge(S["xmax_all"], 1)
            st.then(dve.tensor_scalar(sc[:, XG], sc[:, XALL], 1e-30, 1.0 / F16_TOP, ALU.max, ALU.mult))
            st.sync()
            st.then(dve.tensor_copy(sc[:, ISX], sc[:, XG]))
            dve.reciprocal(sc[:, SX], sc[:, XG]).then_inc(S["sx_ready"], 1)
            dve.wait_ge(S["sx_ready"], 1)

            def weight_columns():
                dve.wait_ge(S["wts_in"], 16 * WTS)
                for k in range(KD):
                    for c in range(2):
                        st.then(dve.scalar_tensor_tensor(out=wsum[:, 0:D], in0=wp[:, k, WG:WC], scalar=1.0,
                                                         in1=asab[:, c * D:(c + 1) * D], op0=ALU.mult, op1=ALU.mult,
                                                         accum_out=wp[:, k, GC + 2 + c:GC + 3 + c]))
                        st.sync()
                flat = lambda a: a.rearrange("p k c -> p (k c)")
                st.then(dve.tensor_tensor(flat(wsq[:]), flat(wp[:]), flat(wp[:]), ALU.mult))
                st.sync()
                dve.tensor_tensor(wsq[:, 1, :], wsq[:, 0, :], wsq[:, 1, :], ALU.add).then_inc(S["wsq_ready"], 1)

            def weight_norm():
                dve.wait_ge(S["wsum_ready"], 1)
                st.then(dve.tensor_reduce(sc[:, TMP], wsum[:], AX, ALU.max))
                st.sync()
                dve.tensor_scalar(sc[:, WMX], sc[:, TMP], 1e-30, None, ALU.max).then_inc(S["wnorm_ready"], 1)

            def weight_scale():
                dve.wait_ge(S["alpha_pow"], 1)
                st.then(dve.tensor_scalar(sc[:, AL], sc[:, WN], F16_TOP / D ** 0.5, None, ALU.mult))
                st.sync()
                st.then(dve.reciprocal(sc[:, IAL], sc[:, AL]))
                st.sync()
                st.then(dve.tensor_scalar(sc[:, HINVA], sc[:, IAL], 0.5 / EDGE_VAL, None, ALU.mult))
                st.then(dve.tensor_scalar(sc[:, EXS], sc[:, IAL], 1.0 / PROJ, None, ALU.mult))
                st.then(dve.tensor_scalar(sc[:, QSC], sc[:, IAL], -SLOPE / PROJ, None, ALU.mult))
                st.then(dve.tensor_scalar(sc[:, WS], sc[:, AL], D ** 0.5, None, ALU.mult))
                st.sync()
                st.then(dve.tensor_scalar(wps[:, :, 0, :], wp[:], sc[:, WS], None, ALU.mult))
                st.sync()
                dve.scalar_tensor_tensor(out=wps[:, :, 1, :], in0=wp[:], scalar=sc[:, WS], in1=wps[:, :, 0, :],
                                         op0=ALU.mult, op1=ALU.subtract).then_inc(S["wps_ready"], 1)
                st.then(dve.tensor_scalar(sc[:, QB], sc[:, IAL], -SLOPE * F16_TOP, None, ALU.mult))
                dve.tensor_scalar(sc[:, INVA], sc[:, IAL], 1.0 / EDGE_VAL, None, ALU.mult).then_inc(S["alpha_ready"], 1)

            for jb in range(T):
                if jb == 0:
                    dve.wait_ge(S["first_in"], 16)
                else:
                    dve.wait_ge(strip_in[jb % RING], 16 * (jb // RING + 1))
                panels = LOWP // 2 if jb == 0 else LOWP
                dve.scalar_tensor_tensor(out=res[:, 0:panels, jb, :],
                                         in0=strip[:, jb % RING, 0:panels * PW].rearrange("p (k i) -> p k i", i=PW),
                                         scalar=float(EDGE - NONE), op0=ALU.mult, op1=ALU.add,
                                         in1=sc[:, CNONE].unsqueeze(2).to_broadcast([P, panels, PW]),
                                         accum_out=degv[:, jb:jb + 1]).then_inc(S["lo_cast"], 1)
                dve.wait_ge(S["yhi_ready"], jb + 1)
                dve.scalar_tensor_tensor(out=y[:, jb, 1, :], in0=xs[:, jb, :], scalar=sc[:, SX],
                                         in1=y[:, jb, 0, :], op0=ALU.mult, op1=ALU.subtract
                                         ).then_inc(S["ylo_ready"], 1)

            def evac(g, dh):
                dve.tensor_copy(acct[g][:, dh, :], ps[:, sum_bank(g, dh), :]).then_inc(S["evac_dve"], 1)

            dve.wait_ge(S["strip_used"], T)
            for dh in range(KD):
                for g in (1, 3):
                    evac(g, dh)
            weight_columns()
            weight_norm()
            weight_scale()
            dve.wait_ge(S["hi_cast"], T)
            dve.wait_ge(S["lo_cast"], T)
            dve.wait_ge(S["first_cast"], 1)
            st.then(dve.tensor_tensor(degv[:, 0:1], degv[:, 0:1], sc[:, DFIRST], ALU.add))
            st.sync()
            st.then(dve.tensor_tensor(deg[:], degv[:], dega[:], ALU.add))
            st.sync()
            st.then(dve.tensor_scalar(deg[:], deg[:], float(-N * NONE), 1.0 / (EDGE - NONE), ALU.add, ALU.mult))
            st.sync()
            st.then(dve.tensor_scalar(deg[:], deg[:], 1.0, None, ALU.max))
            st.sync()
            st.then(dve.tensor_scalar(zs[:], deg[:], 1.0, sc[:, SX], ALU.add, ALU.mult))
            st.then(dve.reciprocal(us[:], deg[:]))
            st.sync()
            st.then(dve.tensor_scalar(zs[:], zs[:], EDGE_VAL, None, ALU.mult))
            dve.tensor_scalar(us[:], us[:], sc[:, ISX], 1.0 / EDGE_VAL, ALU.mult, ALU.mult
                              ).then_inc(S["scale_ready"], 1)
            dve.wait_ge(S["scale_ready"], 1)

            def add_share(t):
                g, tt = t // TG, t % TG
                a = acct[g][:, :, tt * P:(tt + 1) * P]
                dve.wait_ge(S["evac_act"], 8 if g >= NG2 else 4)
                dve.wait_ge(S["evac_dve"], 8 if g >= NG2 else 4)
                dve.wait_ge(S["share_t_done"], t + 1)
                dve.tensor_tensor(a, a, ps[:, BZ, 0:D].rearrange("p (k i) -> p k i", k=KD), ALU.add
                                  ).then_inc(S["sums_ready"], 1)

            def g_lo(t):
                dve.wait_ge(S["ghi_ready"], t + 1)
                dve.scalar_tensor_tensor(out=fa[:, t, 1, :], in0=ps[:, BG(t), 0:GC], scalar=1.0 / PROJ,
                                         in1=fa[:, t, 0, :], op0=ALU.mult, op1=ALU.subtract
                                         ).then_inc(S["glo_ready"], 1)

            def h_lo(t):
                dve.wait_ge(S["hhi_ready"], t + 1)
                dve.scalar_tensor_tensor(out=fb[:, t, 1, 0:D], in0=ps[:, BH(t), 0:D], scalar=qa[:, t:t + 1],
                                         in1=fb[:, t, 0, 0:D], op0=ALU.mult, op1=ALU.subtract
                                         ).then_inc(S["hlo_ready"], 1)

            def x1t_lo(t):
                dve.wait_ge(S["x1t_ready"], t + 1)
                dve.scalar_tensor_tensor(out=x1t[:, t % 2, 1, :], in0=ps[:, BT, 0:D], scalar=X1S,
                                         in1=x1t[:, t % 2, 0, :], op0=ALU.mult, op1=ALU.subtract
                                         ).then_inc(S["x1t_lo_ready"], 1)

            def evac_last(g, dh):
                dve.wait_ge(S["bank_done"], nth_bank(g, dh))
                evac(g, dh)

            evac_last(5, 0)
            add_share(0)
            evac_last(5, 1)
            for n in range(T):
                e = n % 2
                u = ps[:, BU(n), 0:D]
                ln = lnst[:, e, :]
                if n >= 2:
                    x1t_lo(n - 2)
                dve.wait_ge(S["u_done"], n + 1)
                st.then(dve.scalar_tensor_tensor(out=u, in0=u, scalar=us[:, n:n + 1], in1=b0b[:], op0=ALU.mult,
                                                 op1=ALU.add))
                if n >= 3:
                    g_lo(n - 3)
                st.sync()
                dve.scalar_tensor_tensor(out=xs[:, n, :], in0=u, scalar=0.0, in1=xs[:, n, :], op0=ALU.max,
                                         op1=ALU.add).then_inc(S["r_ready"], 1)
                if n < T - 1:
                    add_share(n + 1)
                dve.wait_ge(S["r_ready"], n + 1)
                if n >= 2:
                    dve.wait_ge(S["x1_ready"], n - 1)
                st.then(dve.bn_stats(ln[:, BN], xs[:, n, :]))
                if n >= 3:
                    h_lo(n - 3)
                st.sync()
                st.then(dve.bn_aggr(ln[:, MV], ln[:, BN]))
                st.sync()
                dve.tensor_scalar(ln[:, VE], ln[:, 7:8], EPS, None, ALU.add).then_inc(S["stat_ready"], 1)
                if n in (1, 2):
                    evac_last(7, n - 1)
            for t in range(T - 3, T - 1):
                x1t_lo(t + 1)
                g_lo(t)
                h_lo(t)

            dve.wait_ge(S["ex_ready"], T)
            dve.wait_ge(S["res_out"], 16 * LOWP)
            dve.tensor_scalar(nsr[:], ex[:, :, 3], -1.0, None, ALU.mult).then_inc(S["nsr_ready"], 1)
            dve.wait_ge(S["nsr_ready"], 1)
            dve.tensor_reduce(sc[:, NM], nsr[:], AX, ALU.max).then_inc(S["nsr_max"], 1)
            dve.tensor_copy(slc[:], ex[:, :, 2]).then_inc(S["sl_ready"], 1)
            g_lo(T - 1)
            st.then(dve.tensor_scalar(sr8[:], ex[:, :, 3], float(EDGE), None, ALU.add))
            for k in range(2):
                dve.wait_ge(slb_in[k], 16)
            dve.wait_ge(S["nmax_ready"], 1)
            st.then(dve.tensor_scalar(slb[:], slb[:], sc[:, NMAX], None, ALU.min))
            st.sync()

            def row_factors():
                h_lo(T - 1)
                for c in range(2):
                    st.then(dve.tensor_scalar(rab[:, :, c], ex[:, :, c], sc[:, BAB.start + c:BAB.start + c + 1], 0.5,
                                              ALU.add, ALU.mult))
                dve.wait_ge(S["slt_done"], 1)
                dve.tensor_scalar(slrow[:], ps[0:T, BZ, 0:P], sc[0:T, NMAX], None, ALU.min
                                  ).then_inc(S["slrow_ready"], 1)
                st.then(dve.tensor_scalar(fb[:, :, 0, D], q[:], KAPPA, None, ALU.mult))
                dve.wait_ge(S["sl_ready"], 1)
                st.then(dve.tensor_scalar(ta[:], slc[:], sc[:, NMAX], None, ALU.subtract))
                st.then(dve.tensor_scalar(tb[:], slc[:], SLOPE, sc[:, QB], ALU.mult, ALU.add))
                st.sync()
                st.then(dve.tensor_scalar(ta[:], ta[:], 0.0, 1 - SLOPE, ALU.max, ALU.mult))
                dve.scalar_tensor_tensor(out=fb[:, :, 1, D], in0=q[:], scalar=KAPPA, in1=fb[:, :, 0, D],
                                         op0=ALU.mult, op1=ALU.subtract).then_inc(S["hlo_ready"], 1)
                st.sync()
                dve.tensor_tensor(tb[:], tb[:], ta[:], ALU.add).then_inc(S["arg_ready"], 1)

            def denominators():
                dve.wait_ge(S["rr_ready"], 1)
                st.then(dve.tensor_scalar(rden[:], rr[:], 1.0 / (MU * KAPPA), None, ALU.mult))
                st.then(dve.tensor_scalar(rnum[:], rr[:], sc[:, IAL], 1.0 / MU, ALU.mult, ALU.mult))
                st.sync()

            def relu_chunk(s, slot, c, first=False):
                if not first:
                    gate(dve, S["elow_ready"], s * NCH + c + 1 - ER, "passed_dve")
                for jj in range(CH):
                    jb = c * CH + jj
                    t_ = dve.scalar_tensor_tensor(out=ec[:, c % ER, jj, :], in0=slb[:, slot, :],
                                                  scalar=sr8[:, jb:jb + 1], in1=pan[:, slot, jb, :],
                                                  op0=ALU.add, op1=ALU.max)
                t_.then_inc(S["relu_ready"], 1)

            def low_chunk(s, slot, c):
                gate(dve, S["ehigh_ready"], s * NCH + c + 1, "passed_dve")
                rows = slice(c * CH, (c + 1) * CH)
                dve.scalar_tensor_tensor(out=em[slot][:, 1, rows, :], in0=ec[:, c % ER], scalar=MU,
                                         in1=em[slot][:, 0, rows, :], op0=ALU.mult, op1=ALU.subtract
                                         ).then_inc(S["elow_ready"], 1)

            def panel_waits(slot, nth):
                gate(dve, panel_in[slot], nth * 16, "passed_dve")
                gate(dve, slb_in[slot], nth * 16, "passed_dve")

            of_t = lambda v, t: v[:, bass.ds(t, 1)]

            def epi_w(t, m):
                gate(dve, S["gates_ready"], t + 1, "passed_dve")
                dve.scalar_tensor_tensor(out=w[:, m % 2, :], in0=PA(m)[:, 0:D], scalar=sc[:, INVA], in1=bgb[:],
                                         op0=ALU.mult, op1=ALU.add).then_inc(S["w_ready"], 1)

            def epi_attend(t, m):
                s1 = sc1[:, m % 2, :]
                gate(dve, S["esum_done"], t + 1, "passed_dve")
                st.then(dve.tensor_scalar(s1[:, D2], PH(m)[:, D:D + 1], of_t(rden, t), EPS, ALU.mult, ALU.add))
                st.sync()
                st.then(dve.reciprocal(s1[:, REC], s1[:, D2]))
                st.sync()
                st.then(dve.tensor_scalar(s1[:, CE], s1[:, REC], of_t(rnum, t), s1[:, 10:11], ALU.mult, ALU.mult))
                st.sync()
                gate(dve, S["gated_ready"], t + 1, "passed_dve")
                dve.scalar_tensor_tensor(out=w[:, m % 2, :], in0=PH(m)[:, 0:D], scalar=s1[:, CE],
                                         in1=wb[:, m % 2, :], op0=ALU.mult, op1=ALU.add).then_inc(S["attend_done"], 1)

            def epi_sum(t, m, nth):
                e = m % 2
                s1 = sc1[:, e, :]
                gate(dve, S["sigmoid_ready"], t + 1, "passed_dve")
                gate(dve, x1r_in[e], nth * 16, "passed_dve")
                dve.scalar_tensor_tensor(out=sg[:, e, :], in0=sg[:, e, :], scalar=0.5, in1=x1r[:, e, :],
                                         op0=ALU.mult, op1=ALU.add).then_inc(S["x1r_used"], 1)
                gate(dve, S["x1r_used"], t + 1, "passed_dve")
                st.then(dve.bn_stats(s1[:, BN], sg[:, e, :]))
                gate(dve, S["dve_step"], st.n + st.base, "passed_dve")
                st.then(dve.bn_aggr(s1[:, MV], s1[:, BN]))
                st.sync()
                dve.tensor_scalar(s1[:, VE], s1[:, 7:8], EPS, None, ALU.add).then_inc(S["ystat_ready"], 1)

            def epi_norm(t, m, nth, first=False):
                e = m % 2
                s1 = sc1[:, e, :]
                gate(dve, S["yrstd_ready"], t + 1, "passed_dve")
                if not first:
                    gate(dve, out_sent[e], nth * 16 - 16, "passed_dve")
                dve.tensor_scalar(ot[:, e, :], sg[:, e, :], s1[:, 6:7], s1[:, RS], ALU.subtract, ALU.mult
                                  ).then_inc(S["out_ready"], 1)

            def panel_step(s, m, nth, first=False):
                n = 1 - m
                a, b = s * 2, s * 2 + 1
                panel_waits(n, nth)
                relu_chunk(s + 1, n, 0)
                epi_norm(a - 1, 2 * n + 1, s, first)
                epi_w(a, 2 * m)
                relu_chunk(s + 1, n, 1)
                low_chunk(s + 1, n, 0)
                relu_chunk(s + 1, n, 2)
                epi_attend(a, 2 * m)
                low_chunk(s + 1, n, 1)
                epi_sum(a, 2 * m, s + 1)
                epi_w(b, 2 * m + 1)
                relu_chunk(s + 1, n, 3)
                epi_norm(a, 2 * m, s + 1)
                low_chunk(s + 1, n, 2)
                epi_attend(b, 2 * m + 1)
                low_chunk(s + 1, n, 3)
                epi_sum(b, 2 * m + 1, s + 1)

            for s in range(2):
                gate(dve, panel_in[s], 16, "passed_dve")
                for c in range(NCH):
                    relu_chunk(s, s, c, first=s == 0)
                    if s == 0 and c == 0:
                        row_factors()
                    if c >= 1:
                        low_chunk(s, s, c - 1)
                low_chunk(s, s, NCH - 1)
                if s == 0:
                    denominators()
                    for t in range(2):
                        epi_w(t, t)
            for t in range(2):
                epi_attend(t, t)
                epi_sum(t, t, 1)
            epi_norm(0, 0, 1, first=True)
            panel_step(1, 1, 2, first=True)
            n0 = st.n
            with dve.Fori(1, NPAN // 2 - 1) as k:
                st.n, st.base = n0, k * PER_PAIR - PER_PAIR
                panel_step(k * 2, 0, k + 1)
                panel_step(k * 2 + 1, 1, k + 2)
                assert st.n - n0 == PER_PAIR, st.n - n0
            st.n, st.base = n0 + (NPAN // 2 - 2) * PER_PAIR, 0
            panel_step(NPAN - 2, 0, NPAN // 2)
            epi_norm(T - 3, 1, NPAN - 1)
            for t in range(T - 2, T):
                epi_w(t, t % 4)
            for t in range(T - 2, T):
                epi_attend(t, t % 4)
                epi_sum(t, t % 4, NPAN)
                epi_norm(t, t % 4, NPAN)

        @block.tensor
        def _(pe):
            pe.wait_ge(S["const_ready"], 2)
            pe.wait_ge(x_in[3], 16)
            for _ in range(WARM):
                pe.transpose(ps[:, 0, 0:P], ident[:], ident[:])

            def sums(jb, dh, part, g):
                return pe.matmul(ps[:, sum_bank(g, dh), :], y[:, jb, part, dh * P:(dh + 1) * P],
                                 res[:, 2 * (g % NG2):2 * (g % NG2) + 2, jb, :].bitcast(F8),
                                 start=(jb == 0 and part == 0), stop=(jb == T - 1 and part == 1))

            for jb in range(T):
                pe.wait_ge(S["lo_cast"], jb + 1)
                pe.wait_ge(S["ylo_ready"], jb + 1)
                for groups in ((0, 1), (2, 3)) if jb == 0 else (range(NG2),):
                    if jb == 0 and groups[0] > 0:
                        pe.wait_ge(S["first_cast"], 1)
                    for dh in range(KD):
                        for part in range(2):
                            for g in groups:
                                mm = sums(jb, dh, part, g)
                mm.then_inc(S["strip_used"], 1)
            for jb in range(T - LAST):
                pe.wait_ge(S["hi_cast"], jb + 1)
                for dh in range(KD):
                    for part in range(2):
                        for g in range(NG2, NG):
                            if jb == 0 and part == 0:
                                pe.wait_ge(S["evac_dve" if g % 2 else "evac_act"], 2 * dh + (g - NG2) // 2 + 1)
                            sums(jb, dh, part, g)

            def last_sums(g, dh):
                pe.wait_ge(S["hi_cast"], T)
                for jb in range(T - LAST, T):
                    for part in range(2):
                        mm = sums(jb, dh, part, g)
                mm.then_inc(S["bank_done"], 1)

            def z_step(t):
                pe.wait_ge(S["share_ready"], t + 1)
                if t >= 1:
                    pe.wait_ge(S["sums_ready"], t)
                else:
                    pe.wait_ge(S["evac_dve"], evac_count(5, 0))
                for k in range(KD):
                    mm = pe.transpose(ps[:, BZ, k * P:(k + 1) * P], zx[:, t % 2, k * P:(k + 1) * P], ident[:])
                mm.then_inc(S["share_t_done"], 1)

            def u_step(t):
                g, tt = t // TG, t % TG
                pe.wait_ge(S["sums_ready"], t + 1)
                if t < 2:
                    pe.wait_ge(S["evac_act"], evac_count(4, t))
                else:
                    pe.wait_ge(S["r_ready"], t - 1)
                for k in range(KD):
                    mm = pe.matmul(ps[:, BU(t), 0:D], acct[g][:, k, tt * P:(tt + 1) * P],
                                   w0[:, k, :], start=(k == 0), stop=(k == KD - 1))
                mm.then_inc(S["u_done"], 1)

            def t_step(t):
                pe.wait_ge(S["x1_ready"], t + 1)
                if t >= 1:
                    pe.wait_ge(S["x1t_lo_ready"], t)
                else:
                    pe.wait_ge(S["evac_dve"], evac_count(5, 1))
                for k in range(KD):
                    mm = pe.transpose(ps[:, BT, k * P:(k + 1) * P], xs[:, t, k * P:(k + 1) * P], ident[:])
                mm.then_inc(S["x1t_done"], 1)

            def p_step(t):
                pe.wait_ge(S["x1t_lo_ready"], t + 1)
                if t == 0:
                    pe.wait_ge(S["wps_ready"], 1)
                if t < 2:
                    pe.wait_ge(S["evac_act"], evac_count(6, t))
                    pe.wait_ge(S["evac_dve"], evac_count(7, t))
                else:
                    pe.wait_ge(S["hlo_ready"], t - 1)
                    pe.wait_ge(S["glo_ready"], t - 1)
                for b, c0, c1 in ((BG(t), 0, WG), (BH(t), WG, WC)):
                    for k in range(KD):
                        for x_part, w_part in ((0, 0), (0, 1), (1, 0)):
                            mm = pe.matmul(ps[:, b, 0:c1 - c0], x1t[:, t % 2, x_part, k * P:(k + 1) * P],
                                           wps[:, k, w_part, c0:c1], start=(k == 0 and x_part + w_part == 0),
                                           stop=(k == KD - 1 and x_part == 1))
                mm.then_inc(S["proj_done"], 1)

            def a_rows(m, slot, j0, j1):
                for jb in range(j0, j1):
                    for part in range(2):
                        mm = pe.matmul(PA(m)[:, 0:GC], pan[:, slot, jb, (m % 2) * P:(m % 2 + 1) * P].bitcast(F8),
                                       fa[:, jb, part, :], start=(jb == 0 and part == 0),
                                       stop=(jb == T - 1 and part == 1))
                return mm

            def a_tile(m, slot):
                a_rows(m, slot, 0, T).then_inc(S["asum_done"], 1)

            last_sums(5, 0)
            last_sums(4, 0)
            z_step(0)
            last_sums(5, 1)
            for n in range(T + 2):
                if n < T:
                    u_step(n)
                if n < T - 1:
                    z_step(n + 1)
                if n == 0:
                    last_sums(4, 1)
                    last_sums(6, 0)
                if n == T - 1:
                    pe.wait_ge(panel_in[0], 16)
                    pe.wait_ge(S["glo_ready"], CUTS[1])
                elif n == T:
                    pe.wait_ge(S["r_ready"], T - 1)
                    a_rows(0, 0, 0, CUTS[0])
                elif n == T + 1:
                    a_rows(0, 0, CUTS[0], CUTS[1])
                if n >= 2:
                    p_step(n - 2)
                if 1 <= n <= T:
                    t_step(n - 1)
                if n == 1:
                    last_sums(7, 0)
                    last_sums(6, 1)
                if n == 2:
                    last_sums(7, 1)

            a_rows(0, 0, CUTS[1], CUTS[2])
            pe.wait_ge(S["sl_ready"], 1)
            pe.wait_ge(S["sums_ready"], T)
            pe.transpose(ps[0:T, BZ, 0:P], slc[:], ident[:]).then_inc(S["slt_done"], 1)

            def e_rows(m, slot, j0, j1):
                for jb in range(j0, j1):
                    for e_part, h_part in ((0, 0), (0, 1), (1, 0)):
                        mm = pe.matmul(PH(m)[:, 0:HC], em[slot][:, e_part, jb, (m % 2) * P:(m % 2 + 1) * P],
                                       fb[:, jb, h_part, :], start=(jb == 0 and e_part + h_part == 0),
                                       stop=(jb == T - 1 and e_part == 1))
                return mm

            pe.wait_ge(S["glo_ready"], T)
            a_rows(0, 0, CUTS[2], T).then_inc(S["asum_done"], 1)
            pe.wait_ge(S["r_ready"], T)
            a_tile(1, 0)
            pe.wait_ge(S["slrow_ready"], 1)
            pe.wait_ge(panel_in[1], 16)
            a_tile(2, 1)

            def a_tiles(s, m, nth, first=False):
                if not first:
                    gate(pe, S["w_ready"], s * 2, "passed_pe")
                a_tile(2 * m + 3, 1 - m)
                gate(pe, panel_in[m], nth * 16, "passed_pe")
                gate(pe, S["w_ready"], s * 2 + 1, "passed_pe")
                a_tile(2 * m, m)

            def e_tiles(s, m, first=False):
                gate(pe, S["elow_ready"], s * NCH + NCH, "passed_pe")
                for e in range(2):
                    if not first:
                        gate(pe, S["attend_done"], s * 2 + e - 3, "passed_pe")
                    e_rows(2 * m + e, m, 0, T).then_inc(S["esum_done"], 1)

            pe.wait_ge(S["hlo_ready"], T + 1)
            for c in range(NCH):
                pe.wait_ge(S["elow_ready"], c + 1)
                for e in range(2):
                    mm = e_rows(e, 0, c * CH, (c + 1) * CH)
                    if c == NCH - 1:
                        mm.then_inc(S["esum_done"], 1)
            a_tiles(0, 0, 2, first=True)
            e_tiles(1, 1, first=True)
            a_tiles(1, 1, 2)
            with pe.Fori(1, NPAN // 2 - 1) as k:
                for m in range(2):
                    e_tiles(k * 2 + m, m)
                    a_tiles(k * 2 + m, m, k + 2)
            e_tiles(NPAN - 2, 0)
            pe.wait_ge(S["w_ready"], T - 4)
            a_tile(3, 1)
            e_tiles(NPAN - 1, 1)


_INS = ['x', 'adj', 'L0_gnn_W', 'L0_gnn_b', 'L1_gnn_W_sa', 'L1_gnn_a_sa', 'L1_gnn_W_gcnb', 'L1_gnn_b_gcnb',
        'L1_gnn_Wa', 'L1_gnn_ba', 'L1_gnn_Wb', 'L1_gnn_bb']


def kernel(**inputs):
    import numpy as _np
    import concourse.bacc as _bacc
    from concourse import mybir as _mybir
    from concourse.bass_utils import run_bass_kernel_spmd as _run

    nc = _bacc.Bacc("TRN2", target_bir_lowering=False, num_devices=1)
    arrays, args = {}, []
    for name in _INS:
        a = _np.ascontiguousarray(inputs[name])
        arrays[f"in_{name}_dram"] = a
        args.append(nc.dram_tensor(f"in_{name}_dram", a.shape, _mybir.dt.from_np(a.dtype), kind="ExternalInput").ap())
    o = nc.dram_tensor("out_0_dram", (N, D), _mybir.dt.float32, kind="ExternalOutput").ap()
    build(nc, *args, o)
    r = _run(nc, [arrays], core_ids=[0])
    return r.results[0]["out_0_dram"]
```
